# Optimizing a Trainium2 kernel written in Bass

```python
import numpy as np
import jax
import jax.numpy as jnp

def _softmax(x, axis=-1):
    return jax.nn.softmax(x, axis=axis)

def _gelu(x):
    return jax.nn.gelu(x, approximate=True)

def _silu(x):
    return jax.nn.silu(x)

def _sigmoid(x):
    return jax.nn.sigmoid(x)

def _layernorm(x, axis=-1, eps=1e-05):
    m = jnp.mean(x, axis=axis, keepdims=True)
    v = jnp.var(x, axis=axis, keepdims=True)
    return (x - m) / jnp.sqrt(v + eps)

def _scatter_add(tgt, idx, src, axis=0):
    return tgt.at[idx].add(src)

def _segment_sum(src, seg, n):
    return jax.ops.segment_sum(src, seg, n)
kernel_name = 'mk_adj_resnorm_d4_adj_r2_e2d566'

def setup_inputs(seed: int=0):
    np.random.seed(seed)
    _w = jnp.asarray

    def _rec_inputs():
        import jax
        import jax.numpy as jnp
        _gk = jax.random.key(seed)
        x = -0.0005207 + 1.001 * jax.random.normal(jax.random.fold_in(_gk, 1), (4096, 128), jnp.float32)
        _a = jax.random.bernoulli(jax.random.fold_in(_gk, 2), 0.00195312, (4096, 4096))
        _a = jnp.logical_or(_a, jnp.eye(4096, dtype=bool))
        _af = _a.astype(jnp.float32)
        _af = _af * jax.random.uniform(jax.random.fold_in(_gk, 3), (4096, 4096), jnp.float32, 0.05, 1)
        adj = _af
        return (x, adj)
    x, adj = _rec_inputs()

    def _L0_gnn_setup():
        import jax, jax.numpy as jnp
        import numpy as np
        N = 8192
        IN_DIM = 128
        OUT_DIM = 128

        def _message(X, A, W):
            deg = jnp.sum(A, axis=1, keepdims=True)
            A_norm = A / jnp.where(deg > 0, deg, 1.0)
            return A_norm @ X @ W
        key = jax.random.key(seed)
        k1, k2, k3, k4 = jax.random.split(key, 4)
        X = jax.random.normal(k1, (N, IN_DIM), dtype=jnp.float32)
        A = jax.random.uniform(k2, (N, N), dtype=jnp.float32)
        W_in = jax.random.normal(k3, (IN_DIM, OUT_DIM), dtype=jnp.float32) / np.sqrt(IN_DIM)
        W_out = jax.random.normal(k4, (IN_DIM, OUT_DIM), dtype=jnp.float32) / np.sqrt(IN_DIM)
        return {'X': X, 'A': A, 'W_in': W_in, 'W_out': W_out}
    _L0_gnn_all = _L0_gnn_setup()
    _L0_gnn_in = {k: v for k, v in _L0_gnn_all.items() if k in ('W_in', 'W_out')}
    del _L0_gnn_all

    def _L1_gnn_setup():
        import jax, jax.numpy as jnp
        import numpy as np
        N = 4096
        H = 128
        key = jax.random.key(seed)
        k_x, k_A, k_W = jax.random.split(key, 3)
        x = jax.random.normal(k_x, (N, H), dtype=jnp.float32)
        A = jax.random.uniform(k_A, (N, N), dtype=jnp.float32)
        alpha = jnp.array([0.5], dtype=jnp.float32)
        bound = 1.0 / np.sqrt(H)
        W = jax.random.uniform(k_W, (H, H), dtype=jnp.float32, minval=-bound, maxval=bound)
        b = jnp.zeros((H,), dtype=jnp.float32)
        t = jnp.zeros((1,), dtype=jnp.float32)
        return {'t': t, 'x': x, 'A': A, 'alpha': alpha, 'W': W, 'b': b}
    _L1_gnn_all = _L1_gnn_setup()
    _L1_gnn_in = {k: v for k, v in _L1_gnn_all.items() if k in ('t', 'alpha', 'W', 'b')}
    del _L1_gnn_all

    def _L2_gnn_setup():
        import jax, jax.numpy as jnp
        import numpy as np
        N, D_IN, D_HID, D_OUT, K = (5000, 128, 128, 128, 3)

        def cheb_conv(x, L, W, b):
            Tx0 = x
            out = Tx0 @ W[0]
            Tx1 = L @ x
            out = out + Tx1 @ W[1]
            for k in range(2, W.shape[0]):
                Tx2 = 2.0 * (L @ Tx1) - Tx0
                out = out + Tx2 @ W[k]
                Tx0, Tx1 = (Tx1, Tx2)
            return out + b
        key = jax.random.key(seed)
        ks = jax.random.split(key, 4)
        x = jax.random.normal(ks[0], (N, D_IN), dtype=jnp.float32)
        L = jax.random.normal(ks[1], (N, N), dtype=jnp.float32) / jnp.sqrt(jnp.float32(N))
        W0 = jax.random.normal(ks[2], (K, D_IN, D_HID), dtype=jnp.float32) / jnp.sqrt(jnp.float32(D_IN))
        b0 = jnp.zeros((D_HID,), dtype=jnp.float32)
        W1 = jax.random.normal(ks[3], (K, D_HID, D_OUT), dtype=jnp.float32) / jnp.sqrt(jnp.float32(D_HID))
        b1 = jnp.zeros((D_OUT,), dtype=jnp.float32)
        return {'x': x, 'L': L, 'W0': W0, 'b0': b0, 'W1': W1, 'b1': b1}
    _L2_gnn_all = _L2_gnn_setup()
    _L2_gnn_in = {k: v for k, v in _L2_gnn_all.items() if k in ('W0', 'b0', 'W1', 'b1')}
    del _L2_gnn_all

    def _L3_gnn_setup():
        import jax, jax.numpy as jnp
        import numpy as np
        N = 4096
        F = 128
        AVG_DEGREE = 32
        NEG_INF = -1000000000.0
        LEAKY_ALPHA = 0.3
        EPS = 1e-12

        def _agnn(x, a, beta):
            x_norm = x / jnp.clip(jnp.linalg.norm(x, axis=-1, keepdims=True), EPS, None)
            scores = beta[0] * (x_norm @ x_norm.T)
            scores = jnp.where(a > 0, scores, NEG_INF)
            attn = jax.nn.softmax(scores, axis=-1)
            return attn @ x

        def _leaky(h):
            return jnp.where(h > 0, h, LEAKY_ALPHA * h)
        key = jax.random.key(seed)
        k1, k2 = jax.random.split(key)
        x = jax.random.normal(k1, (N, F), dtype=jnp.float32)
        a = (jax.random.uniform(k2, (N, N)) < AVG_DEGREE / N).astype(jnp.float32)
        a = jnp.maximum(a, jnp.eye(N, dtype=jnp.float32))
        beta1 = jnp.ones((1,), dtype=jnp.float32)
        beta2 = jnp.ones((1,), dtype=jnp.float32)
        return {'x': x, 'a': a, 'beta1': beta1, 'beta2': beta2}
    _L3_gnn_all = _L3_gnn_setup()
    _L3_gnn_in = {k: v for k, v in _L3_gnn_all.items() if k in ('beta1', 'beta2')}
    del _L3_gnn_all
    return {'x': x, 'adj': adj, 'L0_gnn_W_in': _L0_gnn_in['W_in'], 'L0_gnn_W_out': _L0_gnn_in['W_out'], 'L1_gnn_t': _L1_gnn_in['t'], 'L1_gnn_alpha': _L1_gnn_in['alpha'], 'L1_gnn_W': _L1_gnn_in['W'], 'L1_gnn_b': _L1_gnn_in['b'], 'L2_gnn_W0': _L2_gnn_in['W0'], 'L2_gnn_b0': _L2_gnn_in['b0'], 'L2_gnn_W1': _L2_gnn_in['W1'], 'L2_gnn_b1': _L2_gnn_in['b1'], 'L3_gnn_beta1': _L3_gnn_in['beta1'], 'L3_gnn_beta2': _L3_gnn_in['beta2']}

def reference(x, adj, L0_gnn_W_in, L0_gnn_W_out, L1_gnn_t, L1_gnn_alpha, L1_gnn_W, L1_gnn_b, L2_gnn_W0, L2_gnn_b0, L2_gnn_W1, L2_gnn_b1, L3_gnn_beta1, L3_gnn_beta2):
    import jax
    import jax.numpy as jnp

    def _L0_gnn_ref(X, A, W_in, W_out):
        import jax, jax.numpy as jnp
        import numpy as np
        N = 8192
        IN_DIM = 128
        OUT_DIM = 128

        def _message(X, A, W):
            deg = jnp.sum(A, axis=1, keepdims=True)
            A_norm = A / jnp.where(deg > 0, deg, 1.0)
            return A_norm @ X @ W
        X_in = _message(X, A, W_in)
        X_out = _message(X, A.T, W_out)
        return X_in + X_out

    def _L1_gnn_ref(t, x, A, alpha, W, b):
        import jax, jax.numpy as jnp
        import numpy as np
        N = 4096
        H = 128
        a = alpha[0]
        A_prime = a * A
        diag = jnp.diagonal(A_prime) + (1.0 - a)
        A_prime = A_prime.at[jnp.arange(N), jnp.arange(N)].set(diag)
        out_degree = A_prime.sum(axis=1)
        inv_deg = jnp.where(out_degree == 0.0, 0.0, 1.0 / out_degree)
        x = inv_deg[:, None] * A_prime @ x
        x = x @ W.T + b
        return jax.nn.relu(x)

    def _L2_gnn_ref(x, L, W0, b0, W1, b1):
        import jax, jax.numpy as jnp
        import numpy as np
        N, D_IN, D_HID, D_OUT, K = (5000, 128, 128, 128, 3)

        def cheb_conv(x, L, W, b):
            Tx0 = x
            out = Tx0 @ W[0]
            Tx1 = L @ x
            out = out + Tx1 @ W[1]
            for k in range(2, W.shape[0]):
                Tx2 = 2.0 * (L @ Tx1) - Tx0
                out = out + Tx2 @ W[k]
                Tx0, Tx1 = (Tx1, Tx2)
            return out + b
        h = jax.nn.elu(cheb_conv(x, L, W0, b0))
        h = jax.nn.elu(cheb_conv(h, L, W1, b1))
        return h

    def _L3_gnn_ref(x, a, beta1, beta2):
        import jax, jax.numpy as jnp
        import numpy as np
        N = 4096
        F = 128
        AVG_DEGREE = 32
        NEG_INF = -1000000000.0
        LEAKY_ALPHA = 0.3
        EPS = 1e-12

        def _agnn(x, a, beta):
            x_norm = x / jnp.clip(jnp.linalg.norm(x, axis=-1, keepdims=True), EPS, None)
            scores = beta[0] * (x_norm @ x_norm.T)
            scores = jnp.where(a > 0, scores, NEG_INF)
            attn = jax.nn.softmax(scores, axis=-1)
            return attn @ x

        def _leaky(h):
            return jnp.where(h > 0, h, LEAKY_ALPHA * h)
        h = _leaky(_agnn(x, a, beta1))
        h = _leaky(_agnn(h, a, beta2))
        return h
    x = _layernorm(x + _L0_gnn_ref(x, adj, L0_gnn_W_in, L0_gnn_W_out), axis=-1)
    x = _layernorm(x + _L1_gnn_ref(L1_gnn_t, x, adj, L1_gnn_alpha, L1_gnn_W, L1_gnn_b), axis=-1)
    x = _layernorm(x + _L2_gnn_ref(x, adj, L2_gnn_W0, L2_gnn_b0, L2_gnn_W1, L2_gnn_b1), axis=-1)
    x = _layernorm(x + _L3_gnn_ref(x, adj, L3_gnn_beta1, L3_gnn_beta2), axis=-1)
    return x

_drawn_inputs = setup_inputs


def setup_inputs(seed=0):
    import zlib

    import numpy as np

    out = dict(_drawn_inputs(seed))
    spreads = {'L1_gnn_b': (0.0, 0.1), 'L2_gnn_b0': (0.0, 0.355), 'L2_gnn_b1': (0.0, 2.0)}
    factors = {}
    for name, (base, spread) in spreads.items():
        noise = np.random.default_rng([zlib.crc32(name.encode()), seed]).standard_normal(out[name].shape)
        drawn = base * np.exp(spread * noise) if base else spread * noise
        out[name] = jnp.asarray(drawn.astype(out[name].dtype))
    for name, factor in factors.items():
        out[name] = (out[name] * factor).astype(out[name].dtype)
    return out
```

```python
import concourse.bass as bass
from concourse import mybir
from contextlib import ExitStack


def build_gnn_stack(nc, x, adj, w_in, w_out, alpha, w1t, b1, w2a, b2a, w2b, b2b, beta1, beta2, out):
    fp32 = mybir.dt.float32
    bf16 = mybir.dt.bfloat16
    ALU = mybir.AluOpType
    ACT = mybir.ActivationFunctionType
    AX = mybir.AxisListType

    P = 128
    N, D = x.shape
    NT = N // P
    Q = 32
    NA = P // Q
    RANGE = N // NA
    CH = 512
    NCH = N // CH
    TPC = CH // P
    GR = CH // Q
    NQ = 4
    QC = RANGE // NQ
    NU = 2 * NQ
    SETS = QC // Q // 2
    FR = 4
    TR = 4
    OC = N // 2
    OT = 2
    NO = NT // OT
    EPS = 1e-5
    NEG = -1e9
    LEAK = 0.3
    NORM_MIN2 = 1e-24

    KINDS = ["in", "l1", "cheb1", "cheb2", "cheb1", "cheb2f"]
    AGG_DVE = [1, 3, 5]
    X_PASSES = [0, 1, 3, 5]
    LN_PASSES = [0, 1, 5]
    ELU_PASSES = [3, 5]
    FOLD_PASSES = [0, 1, 2, 3, 4]

    def nth(passes, p, k):
        return NCH * passes.index(p) + k

    ctx = ExitStack()
    with ctx:
        def sb(name, shape, dt=fp32):
            return ctx.enter_context(nc.sbuf_tensor(name, shape, dt))

        def sem(name):
            return ctx.enter_context(nc.semaphore(name))

        xn = sb("xn", [P, NT, D])
        xt = sb("xt", [P, N])
        t1t = sb("t1t", [P, N])
        xf = sb("xf", [P, 2, NT, D])
        ring = sb("ring", [P, FR, GR * QC])
        tring = sb("tring", [P, TR, SETS, CH])
        agg_s = sb("agg_s", [P, CH])
        st0 = sb("st0", [P, CH])
        st1 = sb("st1", [P, CH])
        rs = sb("rs", [P, TPC, D])
        ys = sb("ys", [P, TPC, D])
        ns = sb("ns", [P, TPC, D])
        w_in_s = sb("w_in_s", [P, D])
        w_out_s = sb("w_out_s", [P, D])
        w1_s = sb("w1_s", [P, D])
        w2_s = sb("w2_s", [P, 2, 3, D])
        b1_s = sb("b1_s", [P, D])
        b2_s = sb("b2_s", [P, 2, D])
        sc = sb("sc", [P, 3])
        om_a = sb("om_a", [P, 1])
        ident = sb("ident", [P, P])
        ones = sb("ones", [P, 1])
        mhalf = sb("mhalf", [P, TPC])
        rowp = sb("rowp", [P, 2, NT])
        inv_r = sb("inv_r", [P, NT])
        inv_1 = sb("inv_1", [P, NT])
        tmp_a = sb("tmp_a", [P, NT])
        tmp_b = sb("tmp_b", [P, NT])
        inv_c = sb("inv_c", [P, NT // 2])
        stats = sb("stats", [P, TPC, 6])
        mv = sb("mv", [P, TPC, 2])
        var_s = sb("var_s", [P, TPC])
        rstd = sb("rstd", [P, TPC])
        ss = sb("ss", [P, TPC])
        rn = sb("rn", [P, TPC])
        mx = sb("mx", [P, 2, 4])
        nmx = sb("nmx", [P, 4])
        esum = sb("esum", [P, NT])
        rsum = sb("rsum", [P, 2])
        q_s = sb("q_s", [P, 2, P])
        psum = ctx.enter_context(nc.psum_tensor("psum", [P, 8, CH], fp32))

        tflat = tring[:, :, :, :].rearrange("p a b c -> p (a b c)")
        out_s = tflat[:, 0:OC]
        col_s = tflat[:, OC:2 * OC]
        junk = tflat[:, 2 * OC:3 * OC]
        res = t1t[:, :].rearrange("p (t d) -> p t d", d=D)
        PT2 = 2 * P
        pt = tflat.rearrange("p (u i) -> p u i", i=PT2)
        hn = xf[:, 0]

        loaded = [sem(f"loaded{i}") for i in range(FR)]
        consts = sem("consts")
        carried = sem("carried")
        x_in = sem("x_in")
        ident_ready = sem("ident_ready")
        o_pe = sem("o_pe")
        o_act = sem("o_act")
        o_dve = sem("o_dve")
        o_copied = sem("o_copied")
        o_mm = sem("o_mm")
        o_res = sem("o_res")
        dve_step = sem("dve_step")
        pool_step = sem("pool_step")
        transposed = sem("transposed")
        mm_done = sem("mm_done")
        agg_act = sem("agg_act")
        agg_dve = sem("agg_dve")
        y_ready = sem("y_ready")
        y_used = sem("y_used")
        post = sem("post")
        elu_in = sem("elu_in")
        elu_out = sem("elu_out")
        var_ready = sem("var_ready")
        rstd_ready = sem("rstd_ready")
        ss_ready = sem("ss_ready")
        rn_ready = sem("rn_ready")
        ys_ready = sem("ys_ready")
        ns_ready = sem("ns_ready")
        xn_copied = sem("xn_copied")
        folded = sem("folded")
        x_ready = sem("x_ready")
        xt_done = sem("xt_done")
        s_ready = sem("s_ready")
        s_masked = sem("s_masked")
        masked = sem("masked")
        max_ready = sem("max_ready")
        exp_done = sem("exp_done")
        q_ready = sem("q_ready")
        tp_done = sem("tp_done")
        ev_act = sem("ev_act")
        ev_dve = sem("ev_dve")
        pv_done = sem("pv_done")
        o_staged = sem("o_staged")
        ot_ready = sem("ot_ready")
        h_done = sem("h_done")
        h_ready = sem("h_ready")
        hs_ready = sem("hs_ready")
        hss_ready = sem("hss_ready")
        hrn_ready = sem("hrn_ready")
        hn_copied = sem("hn_copied")
        hns_ready = sem("hns_ready")
        hx_ready = sem("hx_ready")
        hxt_done = sem("hxt_done")
        out_ready = sem("out_ready")
        out_done = sem("out_done")
        out_free = sem("out_free")

        def pairs(eng, body):
            body(0, 0)
            body(1, 1)
            with eng.Fori(1, NCH // 2) as m:
                body(m * 2, 0)
                body(m * 2 + 1, 1)

        def before(passes, p, k):
            whole = NCH * len([q for q in passes if q < p])
            return whole + k if p in passes else whole

        def wait_apart(eng, semaphore, value):
            eng.wait_ge(semaphore, value)
            eng.sem_inc(carried, 1)

        def wait_some(eng, semaphore, value):
            if not (isinstance(value, int) and value <= 0):
                eng.wait_ge(semaphore, value)

        def attention(eng, step):
            for tt in range(4):
                step(0, tt, True, tt >= 2, False)
            with eng.Fori(1, NT // 4 - 1) as g:
                for tt in range(4):
                    step(g, tt, True, True, tt % 2 == 0)
            for tt in range(4):
                step(NT // 4 - 1, tt, True, True, tt % 2 == 0)
            step(NT // 4, 0, False, True, True)
            step(NT // 4, 1, False, True, False)
            step(NT // 4, 2, False, False, True)

        def row(ap):
            return ap.rearrange("p a d -> p (a d)")

        class Steps:

            def __init__(self, eng, semaphore, base):
                self.eng, self.semaphore, self.base, self.n = eng, semaphore, base, 0

            def inc(self, instruction):
                instruction.then_inc(self.semaphore, 1)
                self.n += 1

            def wait(self):
                self.eng.wait_ge(self.semaphore, self.base + self.n)

        block = ctx.enter_context(nc.Block())

        @block.sync
        def _(sp):
            for sweep in range(2):
                for n in range(NO):
                    sp.wait_ge(o_pe, sweep * NO + n + 1)
                    sp.wait_ge(o_act, sweep * (OT * NO) + OT * (n + 1))
                    sp.wait_ge(o_dve, sweep * NO + n + 1)
                    src = adj[n * OT * P:(n + 1) * OT * P, sweep * OC:(sweep + 1) * OC]
                    sp.dma_start(ring[:, n % FR, :].rearrange("p (t c) -> p t c", t=OT),
                                 src.rearrange("(t p) c -> p t c", p=P)).then_inc(loaded[n % FR], 16)
            sp.wait_ge(o_pe, 2 * NO + FR)
            sp.wait_ge(o_act, OT * (2 * NO + FR))
            sp.wait_ge(o_dve, 2 * NO + FR)
            for p in range(6):
                with sp.Fori(0, NCH) as k:
                    for h in range(NQ):
                        wait_apart(sp, transposed, k * (2 * NQ) + (2 * NQ * NCH * p + 2 * h + 2))
                        for a in range(NA):
                            c0 = RANGE * a + QC * h
                            src = adj[bass.ds(k * CH, CH), c0:c0 + QC]
                            dst = ring[Q * a:Q * (a + 1), h, :].rearrange("p (g c) -> p g c", c=QC)
                            sp.dma_start(dst, src.rearrange("(g q) c -> q g c", q=Q)).then_inc(loaded[h], 16)
            sp.wait_ge(transposed, 2 * NQ * NCH * 6 + 2 * FR)
            for layer in range(2):
                with sp.Fori(0, NT // 4) as g:
                    for tt in range(4):
                        wait_apart(sp, tp_done, g * 32 + (8 * NT * layer + 8 * tt + 8))
                        sp.dma_start(ring[:, tt, :], adj[bass.ds(g * 4 * P + tt * P, P), :])\
                          .then_inc(loaded[tt], 16)

        N_CONSTS = 11
        LOADS_O = 2 * NO // FR * 16
        LOADS_P = LOADS_O + 6 * NCH * NA * 16

        @block.tensor
        def _(pe):
            pe.sem_inc(o_pe, FR)
            pe.sem_inc(mm_done, TR)
            pe.sem_inc(y_ready, 1)
            pe.sem_inc(o_mm, 1)
            pe.sem_inc(ot_ready, 1)
            pe.sem_inc(tp_done, 8 * FR)
            pe.wait_ge(consts, 16 * N_CONSTS)
            pe.wait_ge(x_in, 16 * (1 + NA))
            pe.wait_ge(ident_ready, 4)
            with pe.Fori(0, 2) as sweep:
                pe.wait_ge(o_res, sweep + 1)
                for n in range(NO):
                    pe.wait_ge(loaded[n % FR], sweep * (LOADS_O // 2) + 16 * (n // FR + 1))
                    tile = ring[:, n % FR, :].rearrange("p (t c) -> p t c", t=OT)
                    for t in range(OT):
                        for c in range(OC // CH):
                            last = nc.tensor.matmul(psum[:, c, :], xn[:, n * OT + t, :],
                                                    tile[:, t, c * CH:(c + 1) * CH],
                                                    start=(n + t == 0), stop=(n == NO - 1 and t == OT - 1))
                    last.then_inc(o_pe, 1)
                pe.wait_ge(o_copied, sweep * 2 + 2)
                for t in range(NT // 2):
                    nc.tensor.matmul(psum[:, t // TPC, t % TPC * D:(t % TPC + 1) * D],
                                     out_s[:, t * P:(t + 1) * P], w_out_s[:, :], start=True, stop=True)
                for t in range(NT // 2):
                    last = nc.tensor.matmul(psum[:, 4, t:t + 1], col_s[:, t * P:(t + 1) * P], ones[:, :],
                                            start=True, stop=True)
                last.then_inc(o_mm, 1)
            pe.wait_ge(o_res, 3)

            for p in range(6):
                kind = KINDS[p]
                if p > 0:
                    pe.wait_ge(folded, 16 * NA * NCH * p)

                def multiply(k, parity, u):
                    pe.wait_ge(transposed, NU * NCH * p + k * NU + u + 1 + 2 * FR)
                    for s in range(SETS):
                        b = u * SETS + s
                        last = nc.tensor.matmul(psum[:, parity, :], xf[:, p % 2, b, :], tring[:, u % TR, s, :],
                                                start=(b == 0), stop=(b == NT - 1))
                    last.then_inc(mm_done, 1)

                def rows(k):
                    pe.wait_ge(agg_act, NCH * p + k + 1)
                    if p in AGG_DVE:
                        pe.wait_ge(agg_dve, nth(AGG_DVE, p, 0) + k + 1)
                    pe.wait_ge(y_used, NCH * p + k + 1)
                    for t in range(TPC):
                        o = psum[:, 2, t * D:(t + 1) * D]
                        cut = slice(t * P, (t + 1) * P)
                        if kind == "in":
                            last = nc.tensor.matmul(o, agg_s[:, cut], w_in_s[:, :], start=True, stop=True)
                        elif kind == "l1":
                            last = nc.tensor.matmul(o, agg_s[:, cut], w1_s[:, :], start=True, stop=True)
                        elif kind == "cheb1":
                            last = nc.tensor.transpose(o, agg_s[:, cut], ident[:, :])
                        else:
                            w = w2_s[:, (p - 3) // 2]
                            nc.tensor.matmul(o, st0[:, cut], w[:, 0, :], start=True, stop=False)
                            nc.tensor.matmul(o, st1[:, cut], w[:, 1, :], start=False, stop=False)
                            last = nc.tensor.matmul(o, agg_s[:, cut], w[:, 2, :], start=False, stop=True)
                    last.then_inc(y_ready, 1)

                def columns(k):
                    if p not in X_PASSES:
                        return
                    src = ys
                    if p == 5:
                        src = ns
                        pe.wait_ge(ns_ready, k + 1)
                    else:
                        pe.wait_ge(ys_ready, NCH * p + k + 1)
                    pe.wait_ge(xt_done, before(X_PASSES, p, k) + 1)
                    for t in range(TPC):
                        last = nc.tensor.transpose(psum[:, 3, t * P:(t + 1) * P], src[:, t, :], ident[:, :])
                    last.then_inc(x_ready, 1)

                def chunk(k, parity):
                    first = isinstance(k, int) and k == 0
                    for u in range(NU):
                        multiply(k, parity, u)
                        if u == 1 and not first:
                            rows(k - 1)
                    if not first:
                        columns(k - 1)

                pairs(pe, chunk)
                rows(NCH - 1)
                columns(NCH - 1)


            pe.wait_ge(xt_done, 4 * NCH + 1)
            pe.wait_ge(xn_copied, 3 * NCH)
            for layer in range(2):
                keys = (xt, t1t)[layer]
                values = (xn[:, :, :], hn)[layer]
                R0 = NT * layer
                G0 = NT // 2 * layer
                if layer == 1:
                    pe.wait_ge(hxt_done, NT // 2 + 1)
                    pe.wait_ge(hn_copied, NT // 2 + 1)

                def step(g, tt, scores, back, pending):
                    if scores:
                        pe.wait_ge(q_ready, g * 4 + (R0 + tt + 1))
                    for q in range(4):
                        if scores:
                            pe.wait_ge(s_masked, g * 16 + (4 * (R0 + tt) + q + 1))
                            for c in range(2):
                                j = (2 * q + c) * CH
                                last = nc.tensor.matmul(psum[:, 2 * (q % 2) + c, :], q_s[:, tt % 2, :],
                                                        keys[:, j:j + CH], start=True, stop=True)
                            last.then_inc(s_ready, 1)
                        if q == 0 and pending:
                            G = g * 2 + (tt // 2 - 2)
                            pe.wait_ge(o_staged, G + (G0 + 1))
                            if layer == 0:
                                pe.wait_ge(hxt_done, G + 1)
                            else:
                                pe.wait_ge(h_ready, G + G0)
                            for t in range(2):
                                last = nc.tensor.transpose(psum[:, 7, t * P:(t + 1) * P],
                                                           agg_s[:, t * P:(t + 1) * P], ident[:, :])
                            last.then_inc(ot_ready, 1)
                        if back:
                            if q == 0:
                                pe.wait_ge(exp_done, g * 4 + (R0 + tt - 1))
                            for w in (2 * q, 2 * q + 1):
                                pe.wait_ge((ev_act, ev_dve)[w % 2], g * 16 + (4 * (R0 + tt - 2) + w // 2 + 1))
                                for i in range(4):
                                    u = 4 * w + i
                                    last = nc.tensor.transpose(psum[:, 4 + w % 2, i * P:(i + 1) * P],
                                                               ring[:, (tt - 2) % 4, u * P:(u + 1) * P], ident[:, :])
                                last.then_inc(tp_done, 1)
                    if pending and layer == 0:
                        pe.wait_ge(hns_ready, g * 2 + (tt // 2 - 1))
                        for t in range(2):
                            last = nc.tensor.transpose(psum[:, 7, PT2 + t * P:PT2 + (t + 1) * P],
                                                       ns[:, t, :], ident[:, :])
                        last.then_inc(hx_ready, 1)
                    if back and tt % 2:
                        pe.wait_ge(ev_act, g * 16 + (4 * (R0 + tt - 1) + 1))
                        pe.wait_ge(ev_dve, g * 16 + (4 * (R0 + tt - 1) + 1))
                        for u in range(NT):
                            last = nc.tensor.matmul(psum[:, 6, 0:PT2], values[:, u, :], pt[:, u, :],
                                                    start=(u == 0), stop=(u == NT - 1))
                        last.then_inc(pv_done, 1)

                attention(pe, step)

        SWEEP_STEPS = NO * OT + 4
        POST_STEPS = {"in": 2, "l1": 3, "cheb1": 0, "cheb2": 1, "cheb2f": 6}
        H_STEPS = (2, 5)

        @block.vector
        def _(ve):
            ve.sem_inc(o_dve, FR)
            ve.sem_inc(o_res, 1)
            ve.sem_inc(transposed, 2 * FR)
            ve.sem_inc(y_used, 1)
            ve.sem_inc(s_masked, 2)
            ve.sem_inc(ev_dve, 1)
            ve.wait_ge(x_in, 16 * (1 + NA))
            ve.wait_ge(consts, 16 * N_CONSTS)
            deg_c = psum[:, 4, 0:NT // 2]
            with ve.Fori(0, 2) as sweep:
                steps = Steps(ve, dve_step, sweep * SWEEP_STEPS)
                acc = psum[:, 4:8, :].rearrange("p b c -> p (b c)")
                for n in range(NO):
                    ve.wait_ge(loaded[n % FR], sweep * (LOADS_O // 2) + 16 * (n // FR + 1))
                    tile = ring[:, n % FR, :].rearrange("p (t c) -> p t c", t=OT)
                    for t in range(OT):
                        if n + t == 0:
                            ins = nc.vector.tensor_copy(acc, tile[:, t, :])
                        else:
                            steps.wait()
                            ins = nc.vector.tensor_tensor(acc, acc, tile[:, t, :], ALU.add)
                        steps.inc(ins)
                    steps.wait()
                    ve.sem_inc(o_dve, 1)
                ve.wait_ge(o_mm, sweep + 2)
                half = slice(0, NT // 2)
                steps.inc(nc.vector.tensor_scalar(tmp_a[:, half], deg_c, 0.0, None, ALU.is_gt))
                steps.wait()
                steps.inc(nc.vector.tensor_tensor(tmp_b[:, half], deg_c, tmp_a[:, half], ALU.mult))
                steps.wait()
                steps.inc(nc.vector.scalar_tensor_tensor(tmp_b[:, half], tmp_b[:, half], 1.0, tmp_a[:, half],
                                                         ALU.add, ALU.subtract))
                steps.wait()
                steps.inc(nc.vector.reciprocal(inv_c[:, :], tmp_b[:, half]))
                steps.wait()
                for t in range(NT // 2):
                    node_tile = bass.ds(sweep * (NT // 2) + t, 1)
                    last = nc.vector.scalar_tensor_tensor(
                        row(res[:, node_tile, :]), psum[:, t // TPC, t % TPC * D:(t % TPC + 1) * D],
                        inv_c[:, t:t + 1], row(xn[:, node_tile, :]), ALU.mult, ALU.add)
                last.then_inc(o_res, 1)
            steps = Steps(ve, dve_step, 2 * SWEEP_STEPS)
            ve.wait_ge(o_act, OT * (2 * NO + FR))
            ve.wait_ge(o_res, 3)
            deg = rowp[:, 0, :]
            steps.inc(nc.vector.tensor_tensor(deg, rowp[:, 0, :], rowp[:, 1, :], ALU.add))
            steps.inc(nc.vector.tensor_scalar(om_a[:, :], sc[:, 0:1], -1.0, 1.0, ALU.mult, ALU.add))
            steps.wait()
            steps.inc(nc.vector.tensor_scalar(tmp_a[:, :], deg, 0.0, None, ALU.is_gt))
            steps.wait()
            steps.inc(nc.vector.tensor_tensor(tmp_b[:, :], deg, tmp_a[:, :], ALU.mult))
            steps.wait()
            steps.inc(nc.vector.scalar_tensor_tensor(tmp_b[:, :], tmp_b[:, :], 1.0, tmp_a[:, :],
                                                     ALU.add, ALU.subtract))
            steps.wait()
            steps.inc(nc.vector.reciprocal(inv_r[:, :], tmp_b[:, :]))
            steps.wait()
            steps.inc(nc.vector.tensor_scalar(tmp_b[:, :], deg, sc[:, 0:1], om_a[:, :], ALU.mult, ALU.add))
            steps.wait()
            steps.inc(nc.vector.tensor_scalar(tmp_a[:, :], tmp_b[:, :], 0.0, None, ALU.is_equal))
            steps.wait()
            steps.inc(nc.vector.tensor_tensor(tmp_b[:, :], tmp_b[:, :], tmp_a[:, :], ALU.add))
            steps.wait()
            steps.inc(nc.vector.reciprocal(inv_1[:, :], tmp_b[:, :]))
            steps.inc(nc.vector.tensor_scalar(tmp_a[:, :], tmp_a[:, :], -1.0, 1.0, ALU.mult, ALU.add))
            steps.wait()
            steps.inc(nc.vector.tensor_tensor(inv_1[:, :], inv_1[:, :], tmp_a[:, :], ALU.mult))
            steps.wait()

            def moments(steps, src, tiles):
                for t in range(tiles):
                    last = nc.vector.bn_stats(stats[:, t, :], src[:, t, :])
                steps.inc(last)
                wait_apart(ve, steps.semaphore, steps.base + steps.n)
                for t in range(tiles):
                    last = nc.vector.bn_aggr(mv[:, t, :], stats[:, t, :])
                steps.inc(last)
                steps.wait()
                nc.vector.tensor_scalar(var_s[:, 0:tiles], mv[:, 0:tiles, 1], EPS, None, ALU.add).then_inc(var_ready, 1)

            post_base = 0
            for p in range(6):
                kind = KINDS[p]

                def transpose(k, u):
                    if u % 2 == 0:
                        ve.wait_ge(loaded[u // 2], LOADS_O + 16 * NA * (NCH * p + 1) + k * (16 * NA))
                    ve.wait_ge(mm_done, NU * NCH * p + k * NU + u + 1)
                    src = ring[:, u // 2, :].rearrange("p (g b q) -> p g b q", g=GR, q=Q)
                    src = src[:, :, u % 2 * SETS:(u % 2 + 1) * SETS, :]
                    dst = tring[:, u % TR].rearrange("p b (g q) -> p g b q", q=Q)
                    nc.vector.transpose(dst, src).then_inc(transposed, 1)

                def aggregate(k, parity):
                    if p not in AGG_DVE:
                        return
                    ve.wait_ge(xt_done, before(X_PASSES, p, 0) + 1)
                    cut = bass.ds(k * CH, CH)
                    if kind == "l1":
                        ve.wait_ge(agg_act, k + (NCH * p + 1))
                        ins = nc.vector.scalar_tensor_tensor(agg_s[:, :], xt[:, cut], om_a[:, :], agg_s[:, :],
                                                             ALU.mult, ALU.add)
                    else:
                        ve.wait_ge(mm_done, k * NU + (NU * (NCH * p + 1) + TR))
                        ve.wait_ge(y_ready, k + (NCH * p + 1))
                        ins = nc.vector.scalar_tensor_tensor(agg_s[:, :], psum[:, parity, :], 2.0, xt[:, cut],
                                                             ALU.mult, ALU.subtract)
                    ins.then_inc(agg_dve, 1)

                def ys_free(k):
                    wait_some(ve, xn_copied, before(LN_PASSES, p, k))
                    wait_some(ve, folded, before(FOLD_PASSES, p, k) * (16 * NA))
                    wait_some(ve, x_ready, before(X_PASSES, p, k))

                def layernorm(k, p_index, src):
                    ve.wait_ge(rstd_ready, k + (p_index + 1))
                    for t in range(TPC):
                        last = nc.vector.tensor_scalar(ys[:, t, :], src[:, t, :], mv[:, t, 0:1], rstd[:, t:t + 1],
                                                       ALU.subtract, ALU.mult)
                    last.then_inc(ys_ready, 1)

                def epilogue(k, stage):
                    if stage == 0:
                        state[0] = Steps(ve, post, k * POST_STEPS[kind] + post_base)
                    steps = state[0]
                    chunk = bass.ds(k * TPC, TPC)
                    seen = k + (NCH * p + 2)
                    if stage == 0:
                        ve.wait_ge(y_ready, seen)
                        if kind == "in":
                            for t in range(TPC):
                                tile = bass.ds(k * TPC + t, 1)
                                last = nc.vector.scalar_tensor_tensor(
                                    rs[:, t, :], psum[:, 2, t * D:(t + 1) * D], inv_r[:, tile],
                                    row(res[:, tile, :]), ALU.mult, ALU.add)
                            last.then_inc(y_used, 1)
                            ve.wait_ge(y_used, seen)
                            moments(steps, rs, TPC)
                        elif kind == "l1":
                            for t in range(TPC):
                                tile = bass.ds(k * TPC + t, 1)
                                last = nc.vector.scalar_tensor_tensor(
                                    rs[:, t, :], psum[:, 2, t * D:(t + 1) * D], inv_1[:, tile], b1_s[:, :],
                                    ALU.mult, ALU.add)
                            last.then_inc(y_used, 1)
                            ve.wait_ge(y_used, seen)
                            steps.inc(nc.vector.scalar_tensor_tensor(rs[:, :, :], rs[:, :, :], 0.0,
                                                                     xn[:, chunk, :], ALU.max, ALU.add))
                            steps.wait()
                            moments(steps, rs, TPC)
                        elif kind == "cheb1":
                            ys_free(k)
                            nc.vector.tensor_copy(ys[:, :, :].rearrange("p t d -> p (t d)"), psum[:, 2, :])\
                              .then_inc(ys_ready, 1)
                            ve.wait_ge(ys_ready, k + (NCH * p + 1))
                            ve.sem_inc(y_used, 1)
                        else:
                            for t in range(TPC):
                                last = nc.vector.tensor_tensor(rs[:, t, :], psum[:, 2, t * D:(t + 1) * D],
                                                               b2_s[:, (p - 3) // 2, :], ALU.add)
                            last.then_inc(y_used, 1)
                            ve.wait_ge(y_used, seen)
                            if p == 5:
                                wait_some(ve, x_ready, before(X_PASSES, p, k))
                            nc.vector.tensor_scalar(ns[:, :, :], rs[:, :, :], 0.0, None, ALU.min).then_inc(elu_in, 1)
                            ve.wait_ge(elu_in, k + (before(ELU_PASSES, p, 0) + 1))
                            steps.inc(nc.vector.tensor_scalar(rs[:, :, :], rs[:, :, :], 0.0, None, ALU.max))
                    elif stage == 1:
                        if kind in ("in", "l1"):
                            ys_free(k)
                            layernorm(k, before(LN_PASSES, p, 0), rs)
                        elif kind == "cheb2":
                            ys_free(k)
                            steps.wait()
                            ve.wait_ge(elu_out, k + (before(ELU_PASSES, p, 0) + 1))
                            nc.vector.scalar_tensor_tensor(ys[:, :, :], ns[:, :, :], -1.0, rs[:, :, :],
                                                           ALU.add, ALU.add).then_inc(ys_ready, 1)
                        elif kind == "cheb2f":
                            steps.wait()
                            ve.wait_ge(elu_out, k + (before(ELU_PASSES, p, 0) + 1))
                            steps.inc(nc.vector.scalar_tensor_tensor(rs[:, :, :], ns[:, :, :], -1.0, rs[:, :, :],
                                                                     ALU.add, ALU.add))
                            steps.wait()
                            steps.inc(nc.vector.tensor_tensor(rs[:, :, :], rs[:, :, :], xn[:, chunk, :], ALU.add))
                            steps.wait()
                            moments(steps, rs, TPC)
                    elif stage == 2 and kind == "cheb2f":
                        ys_free(k)
                        layernorm(k, before(LN_PASSES, p, 0), rs)
                        ve.wait_ge(ys_ready, k + (NCH * p + 1))
                        for t in range(TPC):
                            last = nc.vector.tensor_tensor_reduce(out=rs[:, t, :], in0=ys[:, t, :], in1=ys[:, t, :],
                                                                  scale=1.0, scalar=0.0, op0=ALU.mult, op1=ALU.add,
                                                                  accum_out=ss[:, t:t + 1])
                        steps.inc(last)
                        steps.wait()
                        nc.vector.tensor_scalar(ss[:, :], ss[:, :], NORM_MIN2, None, ALU.max).then_inc(ss_ready, 1)
                    elif stage == 3:
                        if kind == "cheb2f":
                            ve.wait_ge(rn_ready, k + 1)
                            for t in range(TPC):
                                last = nc.vector.tensor_scalar(ns[:, t, :], ys[:, t, :], rn[:, t:t + 1], None, ALU.mult)
                            last.then_inc(ns_ready, 1)
                        assert steps.n == POST_STEPS[kind], (kind, steps.n)

                state = [None]

                def chunk(k, parity):
                    first = isinstance(k, int) and k == 0
                    for u in range(NU):
                        transpose(k, u)
                        if u == 1 and not first:
                            aggregate(k - 1, 1 - parity)
                        if 3 <= u <= 6 and not first:
                            epilogue(k - 1, u - 3)

                pairs(ve, chunk)
                aggregate(NCH - 1, 1)
                for stage in range(4):
                    epilogue(NCH - 1, stage)
                post_base += NCH * POST_STEPS[kind]

            ve.wait_ge(xn_copied, 3 * NCH)
            ve.wait_ge(x_ready, 4 * NCH)
            h_base = 0
            for layer in range(2):
                R0 = NT * layer
                G0 = NT // 2 * layer

                def mask(g, tt):
                    ve.wait_ge(loaded[tt], LOADS_P + 16 * (NT // 4 * layer + 1) + g * 16)
                    nc.vector.tensor_scalar(ring[:, tt, :], ring[:, tt, :], 0.0, NEG, ALU.is_le, ALU.mult)\
                      .then_inc(masked, 1)

                def finish(g, tt):
                    G = g * 2 + (tt // 2 - 2)
                    steps = Steps(ve, h_done, G * H_STEPS[layer] + h_base)
                    ve.wait_ge(ot_ready, G + (G0 + 2))
                    steps.inc(nc.vector.reciprocal(rsum[:, :], esum[:, bass.ds(G * 2, 2)]))
                    steps.wait()
                    for t in range(2):
                        last = nc.vector.tensor_scalar(rs[:, t, :], psum[:, 7, t * D:(t + 1) * D],
                                                       rsum[:, t:t + 1], None, ALU.mult)
                    last.then_inc(h_ready, 1)
                    ve.wait_ge(h_ready, G + (G0 + 1))
                    if layer == 0:
                        ve.wait_ge(hn_copied, G + 1)
                        nc.vector.scalar_tensor_tensor(ys[:, 0:2, :], rs[:, 0:2, :], LEAK, rs[:, 0:2, :],
                                                       ALU.mult, ALU.max).then_inc(hs_ready, 1)
                        ve.wait_ge(hs_ready, G + 1)
                        for t in range(2):
                            last = nc.vector.tensor_tensor_reduce(out=rs[:, t, :], in0=ys[:, t, :], in1=ys[:, t, :],
                                                                  scale=1.0, scalar=0.0, op0=ALU.mult, op1=ALU.add,
                                                                  accum_out=ss[:, t:t + 1])
                        steps.inc(last)
                        steps.wait()
                        nc.vector.tensor_scalar(ss[:, 0:2], ss[:, 0:2], NORM_MIN2, None, ALU.max)\
                          .then_inc(hss_ready, 1)
                        ve.wait_ge(hrn_ready, G + 1)
                        for t in range(2):
                            last = nc.vector.tensor_scalar(ns[:, t, :], ys[:, t, :], rn[:, t:t + 1], None, ALU.mult)
                        last.then_inc(hns_ready, 1)
                    else:
                        steps.inc(nc.vector.scalar_tensor_tensor(ys[:, 0:2, :], rs[:, 0:2, :], LEAK, rs[:, 0:2, :],
                                                                 ALU.mult, ALU.max))
                        steps.wait()
                        steps.inc(nc.vector.tensor_tensor(ys[:, 0:2, :], ys[:, 0:2, :], xn[:, bass.ds(G * 2, 2), :],
                                                          ALU.add))
                        steps.wait()
                        moments(steps, ys, 2)
                        ve.wait_ge(rstd_ready, G + (3 * NCH + 1))
                        ve.wait_ge(out_free, G + 1)
                        for t in range(2):
                            last = nc.vector.tensor_scalar(ns[:, t, :], ys[:, t, :], mv[:, t, 0:1], rstd[:, t:t + 1],
                                                           ALU.subtract, ALU.mult)
                        last.then_inc(out_ready, 1)
                    assert steps.n == H_STEPS[layer], steps.n

                def step(g, tt, scores, back, pending):
                    if scores:
                        ve.wait_ge(masked, g * 4 + (R0 + tt + 1))
                    for q in range(4):
                        if scores:
                            wait_apart(ve, s_ready, g * 16 + (4 * (R0 + tt) + q + 1))
                            b = 2 * (q % 2)
                            part = ring[:, tt, q * 2 * CH:(q + 1) * 2 * CH]
                            nc.vector.tensor_tensor_reduce(
                                out=part, in0=psum[:, b:b + 2, :].rearrange("p b c -> p (b c)"), in1=part,
                                scale=1.0, scalar=-3e38, op0=ALU.add, op1=ALU.max,
                                accum_out=mx[:, tt % 2, q:q + 1]).then_inc(s_masked, 1)
                        if back:
                            w = 2 * q + 1
                            ve.wait_ge(tp_done, g * 32 + (8 * (R0 + tt - 2) + w + 1 + 8 * FR))
                            nc.vector.tensor_copy(pt[:, 4 * w:4 * w + 4, tt % 2 * P:(tt % 2 + 1) * P],
                                                  psum[:, 5, :].rearrange("p (u i) -> p u i", i=P)).then_inc(ev_dve, 1)
                        if pending and q == 1:
                            finish(g, tt)
                    if scores:
                        ve.wait_ge(s_masked, g * 16 + (4 * (R0 + tt) + 6))
                        nc.vector.tensor_reduce(out=nmx[:, tt:tt + 1], in_=mx[:, tt % 2, :], axis=AX.X, op=ALU.max,
                                                negate=True).then_inc(max_ready, 1)
                        if not (isinstance(g, int) and g * 4 + tt == NT - 1):
                            if tt < 3:
                                mask(g, tt + 1)
                            else:
                                mask_next(g)

                def mask_next(g):
                    mask(g + 1, 0)

                mask(0, 0)
                attention(ve, step)
                h_base += NT // 2 * H_STEPS[layer]

        @block.scalar
        def _(act):
            act.sem_inc(o_act, OT * FR)
            act.sem_inc(xt_done, 1)
            act.sem_inc(ev_act, 1)
            act.sem_inc(hxt_done, 1)
            act.dma_start(xn[:, :, :], x.rearrange("(t p) d -> p t d", p=P)).then_inc(x_in, 16)
            for a in range(NA):
                act.dma_start(xf[Q * a:Q * (a + 1), 0], x[RANGE * a:RANGE * (a + 1), :]
                              .rearrange("(b q) d -> q b d", q=Q)).then_inc(x_in, 16)
            act.dma_start(w_out_s[:, :], w_out).then_inc(consts, 16)
            act.dma_start(w_in_s[:, :], w_in).then_inc(consts, 16)
            act.dma_start(w1_s[:, :], w1t).then_inc(consts, 16)
            act.dma_start(w2_s[:, 0], w2a.rearrange("j d e -> d j e")).then_inc(consts, 16)
            act.dma_start(w2_s[:, 1], w2b.rearrange("j d e -> d j e")).then_inc(consts, 16)
            act.dma_start(b1_s[:, :], b1.partition_broadcast(P)).then_inc(consts, 16)
            act.dma_start(b2_s[:, 0], b2a.partition_broadcast(P)).then_inc(consts, 16)
            act.dma_start(b2_s[:, 1], b2b.partition_broadcast(P)).then_inc(consts, 16)
            act.dma_start(sc[:, 0:1], alpha.partition_broadcast(P)).then_inc(consts, 16)
            act.dma_start(sc[:, 1:2], beta1.partition_broadcast(P)).then_inc(consts, 16)
            act.dma_start(sc[:, 2:3], beta2.partition_broadcast(P)).then_inc(consts, 16)
            with act.Fori(0, 2) as sweep:
                for n in range(NO):
                    act.wait_ge(loaded[n % FR], sweep * (LOADS_O // 2) + 16 * (n // FR + 1))
                    tile = ring[:, n % FR, :].rearrange("p (t c) -> p t c", t=OT)
                    for t in range(OT):
                        act.wait_ge(o_act, sweep * (OT * NO) + (OT * (FR + n) + t))
                        nc.scalar.activation(junk, tile[:, t, :], ACT.Copy,
                                             accum_out=rowp[:, bass.ds(sweep, 1), n * OT + t:n * OT + t + 1]
                                             .rearrange("p a b -> p (a b)")).then_inc(o_act, 1)
                act.wait_ge(o_mm, sweep + 1)
                act.wait_ge(o_pe, sweep * NO + (NO + FR))
                nc.scalar.activation(out_s, psum[:, 0:4, :].rearrange("p b c -> p (b c)"), ACT.Copy)\
                  .then_inc(o_copied, 1)
                act.wait_ge(o_dve, sweep * NO + (NO + FR))
                nc.scalar.activation(col_s, psum[:, 4:8, :].rearrange("p b c -> p (b c)"), ACT.Copy)\
                  .then_inc(o_copied, 1)
            act.wait_ge(consts, 16 * N_CONSTS)

            for p in range(6):
                kind = KINDS[p]

                def stage(k, parity):
                    cut = bass.ds(k * CH, CH)
                    act.wait_ge(y_ready, k + (NCH * p + 1))
                    if kind in ("cheb2", "cheb2f"):
                        act.wait_ge(xt_done, before(X_PASSES, p, 0) + 1)
                        nc.scalar.activation(st0[:, :], xt[:, cut], ACT.Copy)
                        act.wait_ge(agg_act, NCH * p)
                        nc.scalar.activation(st1[:, :], t1t[:, cut], ACT.Copy).then_inc(agg_act, 1)
                        return
                    act.wait_ge(mm_done, k * NU + (NU * (NCH * p + 1) + TR))
                    if kind == "l1":
                        nc.scalar.activation(agg_s[:, :], psum[:, parity, :], ACT.Identity, scale=sc[:, 0:1])\
                          .then_inc(agg_act, 1)
                    elif kind == "in":
                        nc.scalar.activation(agg_s[:, :], psum[:, parity, :], ACT.Copy).then_inc(agg_act, 1)
                    else:
                        wait_some(act, agg_act, NCH * p)
                        nc.scalar.activation(t1t[:, cut], psum[:, parity, :], ACT.Copy)
                        nc.scalar.activation(agg_s[:, :], psum[:, parity, :], ACT.Copy).then_inc(agg_act, 1)

                def elu(k):
                    if p in ELU_PASSES:
                        act.wait_ge(elu_in, k + (before(ELU_PASSES, p, 0) + 1))
                        nc.scalar.activation(ns[:, :, :], ns[:, :, :], ACT.Exp).then_inc(elu_out, 1)

                def columns(k):
                    if p in X_PASSES:
                        wait_apart(act, x_ready, k + (before(X_PASSES, p, 0) + 1))
                        nc.scalar.activation(xt[:, bass.ds(k * CH, CH)], psum[:, 3, :], ACT.Copy).then_inc(xt_done, 1)

                def chunk(k, parity):
                    stage(k, parity)
                    if not (isinstance(k, int) and k == 0):
                        columns(k - 1)
                    elu(k)

                pairs(act, chunk)
                columns(NCH - 1)

            act.wait_ge(xt_done, 4 * NCH + 1)
            for layer in range(2):
                keys = (xt, t1t)[layer]
                R0 = NT * layer
                G0 = NT // 2 * layer
                if layer == 1:
                    act.wait_ge(hxt_done, NT // 2 + 1)

                def query(g, tt):
                    nc.scalar.activation(q_s[:, tt % 2, :], keys[:, bass.ds(g * (4 * P) + tt * P, P)], ACT.Identity,
                                         scale=sc[:, 1 + layer:2 + layer]).then_inc(q_ready, 1)

                def step(g, tt, scores, back, pending):
                    G = g * 2 + (tt // 2 - 2)
                    if pending:
                        act.wait_ge(pv_done, G + (G0 + 1))
                        act.wait_ge(ot_ready, G + (G0 + 1))
                        nc.scalar.activation(agg_s[:, 0:PT2], psum[:, 6, 0:PT2], ACT.Copy).then_inc(o_staged, 1)
                    if back:
                        for w in (0, 2, 4, 6):
                            act.wait_ge(tp_done, g * 32 + (8 * (R0 + tt - 2) + w + 1 + 8 * FR))
                            nc.scalar.activation(pt[:, 4 * w:4 * w + 4, tt % 2 * P:(tt % 2 + 1) * P],
                                                 psum[:, 4, :].rearrange("p (u i) -> p u i", i=P), ACT.Copy)\
                              .then_inc(ev_act, 1)
                    if pending and layer == 0:
                        wait_apart(act, hx_ready, G + 1)
                        nc.scalar.activation(t1t[:, bass.ds(G * PT2, PT2)], psum[:, 7, PT2:2 * PT2], ACT.Copy)\
                          .then_inc(hxt_done, 1)
                    if scores:
                        act.wait_ge(max_ready, g * 4 + (R0 + tt + 1))
                        nc.scalar.activation(ring[:, tt, :], ring[:, tt, :], ACT.Exp, bias=nmx[:, tt:tt + 1],
                                             accum_out=esum[:, bass.ds(g * 4 + tt, 1)]).then_inc(exp_done, 1)
                        if tt < 3:
                            query(g, tt + 1)
                        elif not (isinstance(g, int) and g == NT // 4 - 1):
                            query_next(g)

                def query_next(g):
                    query(g + 1, 0)

                query(0, 0)
                attention(act, step)

        @block.gpsimd
        def _(pool):
            nc.gpsimd.memset(ones[:, :], 1.0).then_inc(ident_ready, 1)
            nc.gpsimd.memset(mhalf[:, :], -0.5).then_inc(ident_ready, 1)
            nc.gpsimd.memset(ident[:, :], 0.0).then_inc(ident_ready, 1)
            pool.wait_ge(ident_ready, 3)
            nc.gpsimd.affine_select(out=ident[:, :], in_=ident[:, :], compare_op=ALU.not_equal, fill=1.0,
                                    base=0, pattern=[[-1, P]], channel_multiplier=1).then_inc(ident_ready, 1)
            pool.sem_inc(hn_copied, 1)
            pool.sem_inc(out_free, 1)
            for p in range(6):
                for m in range(NCH // 2):
                    for kk in range(2):
                        if p in LN_PASSES:
                            pool.wait_ge(var_ready, m * 2 + (before(LN_PASSES, p, 0) + kk + 1))
                            nc.gpsimd.tensor_tensor(rstd[:, :], var_s[:, :], mhalf[:, :], ALU.pow)\
                              .then_inc(rstd_ready, 1)
                        pool.wait_ge(ys_ready, m * 2 + (NCH * p + kk + 1))
                        if p in FOLD_PASSES:
                            for s in range(NA):
                                b0 = NT // 2 * kk + s
                                dst = xf[Q * m:Q * (m + 1), (p + 1) % 2, b0:NT // 2 * kk + NT // 2:NA, :]
                                pool.dma_start(dst, ys[Q * s:Q * (s + 1), :, :]).then_inc(folded, 16)
                        if p in LN_PASSES:
                            nc.gpsimd.tensor_copy(xn[:, bass.ds(m * (2 * TPC) + kk * TPC, TPC), :], ys[:, :, :])\
                              .then_inc(xn_copied, 1)
                        if p == 5:
                            pool.wait_ge(ss_ready, m * 2 + (kk + 1))
                            nc.gpsimd.tensor_tensor(rn[:, :], ss[:, :], mhalf[:, :], ALU.pow).then_inc(rn_ready, 1)
            with pool.Fori(0, NT // 2) as G:
                pool.wait_ge(hs_ready, G + 1)
                nc.gpsimd.tensor_copy(hn[:, bass.ds(G * 2, 2), :], ys[:, 0:2, :]).then_inc(hn_copied, 1)
                pool.wait_ge(hss_ready, G + 1)
                nc.gpsimd.tensor_tensor(rn[:, 0:2], ss[:, 0:2], mhalf[:, 0:2], ALU.pow).then_inc(hrn_ready, 1)
            with pool.Fori(0, NT // 2) as G:
                pool.wait_ge(var_ready, G + (3 * NCH + 1))
                nc.gpsimd.tensor_tensor(rstd[:, 0:2], var_s[:, 0:2], mhalf[:, 0:2], ALU.pow).then_inc(rstd_ready, 1)
                pool.wait_ge(out_ready, G + 1)
                pool.dma_start(out[bass.ds(G * (2 * P), 2 * P), :].rearrange("(t p) d -> p t d", p=P),
                               ns[:, 0:2, :]).then_inc(out_done, 16)
                pool.wait_ge(out_done, G * 16 + 16)
                pool.sem_inc(out_free, 1)
    return nc


_INS = ["x", "adj", "L0_gnn_W_in", "L0_gnn_W_out", "L1_gnn_alpha", "L1_gnn_W", "L1_gnn_b",
        "L2_gnn_W0", "L2_gnn_b0", "L2_gnn_W1", "L2_gnn_b1", "L3_gnn_beta1", "L3_gnn_beta2"]


def kernel(**inputs):
    import numpy as np
    import concourse.bacc as bacc
    from concourse import mybir
    from concourse.bass_utils import run_bass_kernel_spmd

    nc = bacc.Bacc("TRN2", target_bir_lowering=False, num_devices=1)
    arrays, args = {}, []
    for name in _INS:
        a = np.asarray(inputs[name])
        if name == "L1_gnn_W":
            a = a.T
        a = np.ascontiguousarray(a)
        arrays[f"in_{name}_dram"] = a
        args.append(nc.dram_tensor(f"in_{name}_dram", a.shape, mybir.dt.from_np(a.dtype),
                                   kind="ExternalInput").ap())
    out = nc.dram_tensor("out_dram", (4096, 128), mybir.dt.float32, kind="ExternalOutput").ap()
    build_gnn_stack(nc, *args, out)
    r = run_bass_kernel_spmd(nc, [arrays], core_ids=[0])
    return r.results[0]["out_dram"]
```

```python
import concourse.bass as bass
from concourse import mybir
from contextlib import ExitStack


def build_gnn_stack(nc, x, adj, w_in, w_out, alpha, w1t, b1, w2a, b2a, w2b, b2b, beta1, beta2, out):
    fp32 = mybir.dt.float32
    fp32r = mybir.dt.float32r
    ALU = mybir.AluOpType
    ACT = mybir.ActivationFunctionType
    AX = mybir.AxisListType

    P = 128
    N, D = x.shape
    NT = N // P
    Q = 32
    NA = P // Q
    RANGE = N // NA
    CH = 512
    NCH = N // CH
    TPC = CH // P
    GR = CH // Q
    NQ = 4
    QC = RANGE // NQ
    NU = 2 * NQ
    SETS = QC // Q // 2
    FR = 4
    TR = 4
    OC = N // 2
    OT = 2
    NO = NT // OT
    EPS = 1e-5
    NEG = -1e9
    LEAK = 0.3
    NORM_MIN2 = 1e-24

    KINDS = ["in", "l1", "cheb1", "cheb2", "cheb1", "cheb2f"]
    AGG_DVE = [1, 3, 5]
    X_PASSES = [0, 1, 3, 5]
    LN_PASSES = [0, 1, 5]
    ELU_PASSES = [3, 5]
    FOLD_PASSES = [0, 1, 2, 3, 4]

    def nth(passes, p, k):
        return NCH * passes.index(p) + k

    ctx = ExitStack()
    with ctx:
        def sb(name, shape, dt=fp32):
            return ctx.enter_context(nc.sbuf_tensor(name, shape, dt))

        def sem(name):
            return ctx.enter_context(nc.semaphore(name))

        sc = sb("sc", [P, 3])
        ident = sb("ident", [P, P])
        mhalf = sb("mhalf", [P, TPC])
        stats = sb("stats", [P, TPC, 6])
        mv = sb("mv", [P, TPC, 2])
        var_s = sb("var_s", [P, TPC])
        rstd = sb("rstd", [P, TPC])
        ss = sb("ss", [P, TPC])
        rn = sb("rn", [P, TPC])
        ring = sb("ring", [P, FR, GR * QC])

        with ExitStack() as passes_ctx:
            def sb_a(name, shape, dt=fp32):
                return passes_ctx.enter_context(nc.sbuf_tensor(name, shape, dt))

            xn = sb_a("xn", [P, NT, D])
            xt = sb_a("xt", [P, N])
            tring = sb_a("tring", [P, TR, SETS, CH])
            xf = sb_a("xf", [P, 2, NT, D])
            t1t = sb_a("t1t", [P, N])
            agg_s = sb_a("agg_s", [P, CH])
            st0 = sb_a("st0", [P, CH])
            st1 = sb_a("st1", [P, CH])
            rs = sb_a("rs", [P, TPC, D])
            ys = sb_a("ys", [P, TPC, D])
            ns = sb_a("ns", [P, TPC, D])
            w_in_s = sb_a("w_in_s", [P, D])
            w_out_s = sb_a("w_out_s", [P, D])
            w1_s = sb_a("w1_s", [P, D])
            w2_s = sb_a("w2_s", [P, 2, 3, D])
            b1_s = sb_a("b1_s", [P, D])
            b2_s = sb_a("b2_s", [P, 2, D])
            om_a = sb_a("om_a", [P, 1])
            ones = sb_a("ones", [P, 1])
            rowp = sb_a("rowp", [P, 2, NT])
            inv_r = sb_a("inv_r", [P, NT])
            inv_1 = sb_a("inv_1", [P, NT])
            tmp_a = sb_a("tmp_a", [P, NT])
            tmp_b = sb_a("tmp_b", [P, NT])
            inv_c = sb_a("inv_c", [P, NT // 2])

        PT2 = 2 * P
        pt_h = sb("pt_h", [P, NT, PT2], fp32r)
        pt_l = sb("pt_l", [P, NT, PT2], fp32r)
        k_h = sb("k_h", [P, N], fp32r)
        k_l = sb("k_l", [P, N], fp32r)
        v_h = sb("v_h", [P, NT, D], fp32r)
        v_l = sb("v_l", [P, NT, D], fp32r)
        o_s = sb("o_s", [P, PT2])
        hr = sb("hr", [P, 2, D])
        hy = sb("hy", [P, 2, D])
        hz = sb("hz", [P, 2, D])
        hk = sb("hk", [P, PT2])
        x3_s = sb("x3_s", [P, 2, D])
        q_f = sb("q_f", [P, 2, P])
        q_h = sb("q_h", [P, 2, P], fp32r)
        q_l = sb("q_l", [P, 2, P], fp32r)
        mx = sb("mx", [P, 2, 4])
        nmx = sb("nmx", [P, 4])
        esum = sb("esum", [P, NT, 4])
        rsum = sb("rsum", [P, 2])

        x3_d = nc.dram_tensor("x3_d", [N, D], fp32, kind="Internal").ap()
        h_d = nc.dram_tensor("h_d", [N, D], fp32, kind="Internal").ap()
        hk_d = nc.dram_tensor("hk_d", [P, N], fp32, kind="Internal").ap()
        psum = ctx.enter_context(nc.psum_tensor("psum", [P, 8, CH], fp32))

        tflat = tring[:, :, :, :].rearrange("p a b c -> p (a b c)")
        out_s = tflat[:, 0:OC]
        col_s = tflat[:, OC:2 * OC]
        junk = tflat[:, 2 * OC:3 * OC]
        res = t1t[:, :].rearrange("p (t d) -> p t d", d=D)
        loaded = [sem(f"loaded{i}") for i in range(FR)]
        consts = sem("consts")
        carried = sem("carried")
        x_in = sem("x_in")
        ident_ready = sem("ident_ready")
        o_pe = sem("o_pe")
        o_act = sem("o_act")
        o_dve = sem("o_dve")
        o_copied = sem("o_copied")
        o_mm = sem("o_mm")
        o_res = sem("o_res")
        dve_step = sem("dve_step")
        pool_step = sem("pool_step")
        transposed = sem("transposed")
        mm_done = sem("mm_done")
        agg_act = sem("agg_act")
        agg_dve = sem("agg_dve")
        y_ready = sem("y_ready")
        y_used = sem("y_used")
        post = sem("post")
        elu_in = sem("elu_in")
        elu_out = sem("elu_out")
        var_ready = sem("var_ready")
        rstd_ready = sem("rstd_ready")
        ss_ready = sem("ss_ready")
        rn_ready = sem("rn_ready")
        ys_ready = sem("ys_ready")
        ns_ready = sem("ns_ready")
        xn_copied = sem("xn_copied")
        folded = sem("folded")
        x_ready = sem("x_ready")
        xt_done = sem("xt_done")
        s_ready = sem("s_ready")
        s_masked = sem("s_masked")
        a_loaded = [[sem(f"a_loaded{i}_{q}") for q in range(4)] for i in range(FR)]
        masked = sem("masked")
        max_ready = sem("max_ready")
        exp_done = sem("exp_done")
        tp_done = sem("tp_done")
        ev_high = sem("ev_high")
        ev_low = sem("ev_low")
        k_high = sem("k_high")
        k_split = sem("k_split")
        v_high = sem("v_high")
        v_split = sem("v_split")
        q_raw = sem("q_raw")
        q_made = sem("q_made")
        qh_ready = sem("qh_ready")
        ql_ready = sem("ql_ready")
        pv_done = sem("pv_done")
        o_staged = sem("o_staged")
        ot_ready = sem("ot_ready")
        h_done = sem("h_done")
        h_ready = sem("h_ready")
        hs_ready = sem("hs_ready")
        hss_ready = sem("hss_ready")
        hrn_ready = sem("hrn_ready")
        h_stored = sem("h_stored")
        hy_free = sem("hy_free")
        hns_ready = sem("hns_ready")
        hx_ready = sem("hx_ready")
        hk_ready = sem("hk_ready")
        hk_stored = sem("hk_stored")
        hk_free = sem("hk_free")
        x3_stored = sem("x3_stored")
        x3_loaded = sem("x3_loaded")
        h_loaded = [sem("hk_loaded"), sem("hv_loaded")]
        out_ready = sem("out_ready")
        out_done = sem("out_done")
        out_free = sem("out_free")

        def pairs(eng, body):
            body(0, 0)
            body(1, 1)
            with eng.Fori(1, NCH // 2) as m:
                body(m * 2, 0)
                body(m * 2 + 1, 1)

        def before(passes, p, k):
            whole = NCH * len([q for q in passes if q < p])
            return whole + k if p in passes else whole

        def wait_apart(eng, semaphore, value):
            eng.wait_ge(semaphore, value)
            eng.sem_inc(carried, 1)

        def wait_some(eng, semaphore, value):
            if not (isinstance(value, int) and value <= 0):
                eng.wait_ge(semaphore, value)

        def attention(eng, step):
            for tt in range(4):
                step(0, tt, True, tt >= 2, False)
            with eng.Fori(1, NT // 4 - 1) as g:
                for tt in range(4):
                    step(g, tt, True, True, True)
            for tt in range(4):
                step(NT // 4 - 1, tt, True, True, True)
            for tt in range(4):
                step(NT // 4, tt, False, tt < 2, True)

        def next_tile(g, tt):
            return (g, tt + 1) if tt < 3 else (g + 1, 0)

        def pt_cut(w, tt):
            return (slice(None), slice(4 * w, 4 * w + 4), slice(tt % 2 * P, (tt % 2 + 1) * P))

        def row(ap):
            return ap.rearrange("p a d -> p (a d)")

        class Steps:

            def __init__(self, eng, semaphore, base):
                self.eng, self.semaphore, self.base, self.n = eng, semaphore, base, 0

            def inc(self, instruction):
                instruction.then_inc(self.semaphore, 1)
                self.n += 1

            def wait(self):
                self.eng.wait_ge(self.semaphore, self.base + self.n)

        block = ctx.enter_context(nc.Block())

        @block.sync
        def _(sp):
            for sweep in range(2):
                for n in range(NO):
                    sp.wait_ge(o_pe, sweep * NO + n + 1)
                    sp.wait_ge(o_act, sweep * (OT * NO) + OT * (n + 1))
                    sp.wait_ge(o_dve, sweep * NO + n + 1)
                    src = adj[n * OT * P:(n + 1) * OT * P, sweep * OC:(sweep + 1) * OC]
                    sp.dma_start(ring[:, n % FR, :].rearrange("p (t c) -> p t c", t=OT),
                                 src.rearrange("(t p) c -> p t c", p=P)).then_inc(loaded[n % FR], 16)
            sp.wait_ge(o_pe, 2 * NO + FR)
            sp.wait_ge(o_act, OT * (2 * NO + FR))
            sp.wait_ge(o_dve, 2 * NO + FR)
            for p in range(6):
                with sp.Fori(0, NCH) as k:
                    for h in range(NQ):
                        wait_apart(sp, transposed, k * (2 * NQ) + (2 * NQ * NCH * p + 2 * h + 2))
                        for a in range(NA):
                            c0 = RANGE * a + QC * h
                            src = adj[bass.ds(k * CH, CH), c0:c0 + QC]
                            dst = ring[Q * a:Q * (a + 1), h, :].rearrange("p (g c) -> p g c", c=QC)
                            sp.dma_start(dst, src.rearrange("(g q) c -> q g c", q=Q)).then_inc(loaded[h], 16)
            sp.wait_ge(transposed, 2 * NQ * NCH * 6 + 2 * FR)
            for layer in range(2):
                if layer == 1:
                    sp.wait_ge(pv_done, NT // 2)
                    sp.wait_ge(hk_stored, 16 * (NT // 2))
                    sp.dma_start(xt[:, :], hk_d).then_inc(h_loaded[0], 16)
                    sp.wait_ge(h_stored, 16 * (NT // 2))
                    sp.dma_start(xn[:, :, :], h_d.rearrange("(t p) d -> p t d", p=P)).then_inc(h_loaded[1], 16)
                with sp.Fori(0, NT // 4) as g:
                    for tt in range(4):
                        for q in range(4):
                            wait_apart(sp, tp_done, g * 32 + (8 * NT * layer + 8 * tt + 2 * q + 2))
                            cut = slice(q * 2 * CH, (q + 1) * 2 * CH)
                            sp.dma_start(ring[:, tt, cut], adj[bass.ds(g * 4 * P + tt * P, P), cut])\
                              .then_inc(a_loaded[tt][q], 16)

        N_CONSTS = 11
        LOADS_O = 2 * NO // FR * 16

        @block.tensor
        def _(pe):
            pe.sem_inc(o_pe, FR)
            pe.sem_inc(mm_done, TR)
            pe.sem_inc(y_ready, 1)
            pe.sem_inc(o_mm, 1)
            pe.sem_inc(ot_ready, 1)
            pe.sem_inc(tp_done, 8 * FR)
            pe.wait_ge(consts, 16 * N_CONSTS)
            pe.wait_ge(x_in, 16 * (1 + NA))
            pe.wait_ge(ident_ready, 4)
            with pe.Fori(0, 2) as sweep:
                pe.wait_ge(o_res, sweep + 1)
                for n in range(NO):
                    pe.wait_ge(loaded[n % FR], sweep * (LOADS_O // 2) + 16 * (n // FR + 1))
                    tile = ring[:, n % FR, :].rearrange("p (t c) -> p t c", t=OT)
                    for t in range(OT):
                        for c in range(OC // CH):
                            last = nc.tensor.matmul(psum[:, c, :], xn[:, n * OT + t, :],
                                                    tile[:, t, c * CH:(c + 1) * CH],
                                                    start=(n + t == 0), stop=(n == NO - 1 and t == OT - 1))
                    last.then_inc(o_pe, 1)
                pe.wait_ge(o_copied, sweep * 2 + 2)
                for t in range(NT // 2):
                    nc.tensor.matmul(psum[:, t // TPC, t % TPC * D:(t % TPC + 1) * D],
                                     out_s[:, t * P:(t + 1) * P], w_out_s[:, :], start=True, stop=True)
                for t in range(NT // 2):
                    last = nc.tensor.matmul(psum[:, 4, t:t + 1], col_s[:, t * P:(t + 1) * P], ones[:, :],
                                            start=True, stop=True)
                last.then_inc(o_mm, 1)
            pe.wait_ge(o_res, 3)

            for p in range(6):
                kind = KINDS[p]
                if p > 0:
                    pe.wait_ge(folded, 16 * NA * NCH * p)

                def multiply(k, parity, u):
                    pe.wait_ge(transposed, NU * NCH * p + k * NU + u + 1 + 2 * FR)
                    for s in range(SETS):
                        b = u * SETS + s
                        last = nc.tensor.matmul(psum[:, parity, :], xf[:, p % 2, b, :], tring[:, u % TR, s, :],
                                                start=(b == 0), stop=(b == NT - 1))
                    last.then_inc(mm_done, 1)

                def rows(k):
                    pe.wait_ge(agg_act, NCH * p + k + 1)
                    if p in AGG_DVE:
                        pe.wait_ge(agg_dve, nth(AGG_DVE, p, 0) + k + 1)
                    pe.wait_ge(y_used, NCH * p + k + 1)
                    for t in range(TPC):
                        o = psum[:, 2, t * D:(t + 1) * D]
                        cut = slice(t * P, (t + 1) * P)
                        if kind == "in":
                            last = nc.tensor.matmul(o, agg_s[:, cut], w_in_s[:, :], start=True, stop=True)
                        elif kind == "l1":
                            last = nc.tensor.matmul(o, agg_s[:, cut], w1_s[:, :], start=True, stop=True)
                        elif kind == "cheb1":
                            last = nc.tensor.transpose(o, agg_s[:, cut], ident[:, :])
                        else:
                            w = w2_s[:, (p - 3) // 2]
                            nc.tensor.matmul(o, st0[:, cut], w[:, 0, :], start=True, stop=False)
                            nc.tensor.matmul(o, st1[:, cut], w[:, 1, :], start=False, stop=False)
                            last = nc.tensor.matmul(o, agg_s[:, cut], w[:, 2, :], start=False, stop=True)
                    last.then_inc(y_ready, 1)

                def columns(k):
                    if p not in X_PASSES:
                        return
                    src = ys
                    if p == 5:
                        src = ns
                        pe.wait_ge(ns_ready, k + 1)
                    else:
                        pe.wait_ge(ys_ready, NCH * p + k + 1)
                    pe.wait_ge(xt_done, before(X_PASSES, p, k) + 1)
                    for t in range(TPC):
                        last = nc.tensor.transpose(psum[:, 3, t * P:(t + 1) * P], src[:, t, :], ident[:, :])
                    last.then_inc(x_ready, 1)

                def chunk(k, parity):
                    first = isinstance(k, int) and k == 0
                    for u in range(NU):
                        multiply(k, parity, u)
                        if u == 1 and not first:
                            rows(k - 1)
                    if not first:
                        columns(k - 1)

                pairs(pe, chunk)
                rows(NCH - 1)
                columns(NCH - 1)


            for layer in range(2):
                R0 = NT * layer
                G0 = NT // 2 * layer
                pe.wait_ge(k_split, 4 * (layer + 1))

                BLOCKS = ({0: 3, 2: 4, 4: 5, 6: 6, 7: 7}, {2: 0, 4: 1, 6: 2})

                def product(block):
                    for u in range(4 * block, 4 * block + 4):
                        for v, probs in ((v_h, pt_h), (v_h, pt_l), (v_l, pt_h)):
                            last = nc.tensor.matmul(psum[:, 6, 0:PT2], v[:, u, :], probs[:, u, :],
                                                    start=(u == 0 and v is v_h and probs is pt_h),
                                                    stop=(u == NT - 1 and v is v_l))
                    if block == 7:
                        last.then_inc(pv_done, 1)

                def step(g, tt, scores, back, ends):
                    if scores:
                        pe.wait_ge(ql_ready, g * 4 + (R0 + tt + 1))
                    for q in range(4):
                        if scores:
                            pe.wait_ge(s_masked, g * 16 + (4 * (R0 + tt) + q + 1))
                            slot = tt % 2
                            for weights, parts in ((q_h, (k_h, k_l)), (q_l, (k_h,))):
                                for c in range(2):
                                    j = (2 * q + c) * CH
                                    for part in parts:
                                        last = nc.tensor.matmul(psum[:, 2 * (q % 2) + c, :], weights[:, slot, :],
                                                                part[:, j:j + CH],
                                                                start=(weights is q_h and part is k_h),
                                                                stop=(weights is q_l), skip_group_check=True)
                            last.then_inc(s_ready, 1)
                        if back and q == 0:
                            pe.wait_ge(exp_done, g * 16 + 4 * (R0 + tt - 1))
                        for w in (2 * q, 2 * q + 1):
                            if w in BLOCKS[tt % 2] and (ends if tt % 2 == 0 else back):
                                block = BLOCKS[tt % 2][w]
                                if block == 0 and isinstance(g, int) and g == 0:
                                    pe.wait_ge(v_split, 2 * (layer + 1))
                                tile_2 = R0 + tt - (2 if tt % 2 else 3)
                                pe.wait_ge(ev_low, g * 32 + (8 * tile_2 + block + 1 + 2))
                                product(block)
                            if back:
                                pe.wait_ge(ev_low, g * 32 + (8 * (R0 + tt - 2) + w + 1))
                                for i in range(4):
                                    u = 4 * w + i
                                    last = nc.tensor.transpose(psum[:, 4 + w % 2, i * P:(i + 1) * P],
                                                               ring[:, (tt - 2) % 4, u * P:(u + 1) * P], ident[:, :])
                                last.then_inc(tp_done, 1)
                            if ends and tt % 2 and w == 1:
                                G = g * 2 + (tt // 2 - 2)
                                pe.wait_ge(o_staged, G + (G0 + 1))
                                if layer == 0:
                                    pe.wait_ge(hk_ready, G + 1)
                                else:
                                    pe.wait_ge(h_ready, G + G0)
                                for t in range(2):
                                    last = nc.tensor.transpose(psum[:, 7, t * P:(t + 1) * P],
                                                               o_s[:, t * P:(t + 1) * P], ident[:, :])
                                last.then_inc(ot_ready, 1)
                    if ends and tt % 2 and layer == 0:
                        pe.wait_ge(hns_ready, g * 2 + (tt // 2 - 1))
                        for t in range(2):
                            last = nc.tensor.transpose(psum[:, 7, PT2 + t * P:PT2 + (t + 1) * P],
                                                       hz[:, t, :], ident[:, :])
                        last.then_inc(hx_ready, 1)

                attention(pe, step)

        SWEEP_STEPS = NO * OT + 4
        POST_STEPS = {"in": 2, "l1": 3, "cheb1": 0, "cheb2": 1, "cheb2f": 6}
        H_STEPS = (3, 6)

        @block.vector
        def _(ve):
            ve.sem_inc(o_dve, FR)
            ve.sem_inc(o_res, 1)
            ve.sem_inc(transposed, 2 * FR)
            ve.sem_inc(y_used, 1)
            ve.sem_inc(s_masked, 2)
            ve.sem_inc(ev_low, 2)
            ve.wait_ge(x_in, 16 * (1 + NA))
            ve.wait_ge(consts, 16 * N_CONSTS)
            deg_c = psum[:, 4, 0:NT // 2]
            with ve.Fori(0, 2) as sweep:
                steps = Steps(ve, dve_step, sweep * SWEEP_STEPS)
                acc = psum[:, 4:8, :].rearrange("p b c -> p (b c)")
                for n in range(NO):
                    ve.wait_ge(loaded[n % FR], sweep * (LOADS_O // 2) + 16 * (n // FR + 1))
                    tile = ring[:, n % FR, :].rearrange("p (t c) -> p t c", t=OT)
                    for t in range(OT):
                        if n + t == 0:
                            ins = nc.vector.tensor_copy(acc, tile[:, t, :])
                        else:
                            steps.wait()
                            ins = nc.vector.tensor_tensor(acc, acc, tile[:, t, :], ALU.add)
                        steps.inc(ins)
                    steps.wait()
                    ve.sem_inc(o_dve, 1)
                ve.wait_ge(o_mm, sweep + 2)
                half = slice(0, NT // 2)
                steps.inc(nc.vector.tensor_scalar(tmp_a[:, half], deg_c, 0.0, None, ALU.is_gt))
                steps.wait()
                steps.inc(nc.vector.tensor_tensor(tmp_b[:, half], deg_c, tmp_a[:, half], ALU.mult))
                steps.wait()
                steps.inc(nc.vector.scalar_tensor_tensor(tmp_b[:, half], tmp_b[:, half], 1.0, tmp_a[:, half],
                                                         ALU.add, ALU.subtract))
                steps.wait()
                steps.inc(nc.vector.reciprocal(inv_c[:, :], tmp_b[:, half]))
                steps.wait()
                for t in range(NT // 2):
                    node_tile = bass.ds(sweep * (NT // 2) + t, 1)
                    last = nc.vector.scalar_tensor_tensor(
                        row(res[:, node_tile, :]), psum[:, t // TPC, t % TPC * D:(t % TPC + 1) * D],
                        inv_c[:, t:t + 1], row(xn[:, node_tile, :]), ALU.mult, ALU.add)
                last.then_inc(o_res, 1)
            steps = Steps(ve, dve_step, 2 * SWEEP_STEPS)
            ve.wait_ge(o_act, OT * (2 * NO + FR))
            ve.wait_ge(o_res, 3)
            deg = rowp[:, 0, :]
            steps.inc(nc.vector.tensor_tensor(deg, rowp[:, 0, :], rowp[:, 1, :], ALU.add))
            steps.inc(nc.vector.tensor_scalar(om_a[:, :], sc[:, 0:1], -1.0, 1.0, ALU.mult, ALU.add))
            steps.wait()
            steps.inc(nc.vector.tensor_scalar(tmp_a[:, :], deg, 0.0, None, ALU.is_gt))
            steps.wait()
            steps.inc(nc.vector.tensor_tensor(tmp_b[:, :], deg, tmp_a[:, :], ALU.mult))
            steps.wait()
            steps.inc(nc.vector.scalar_tensor_tensor(tmp_b[:, :], tmp_b[:, :], 1.0, tmp_a[:, :],
                                                     ALU.add, ALU.subtract))
            steps.wait()
            steps.inc(nc.vector.reciprocal(inv_r[:, :], tmp_b[:, :]))
            steps.wait()
            steps.inc(nc.vector.tensor_scalar(tmp_b[:, :], deg, sc[:, 0:1], om_a[:, :], ALU.mult, ALU.add))
            steps.wait()
            steps.inc(nc.vector.tensor_scalar(tmp_a[:, :], tmp_b[:, :], 0.0, None, ALU.is_equal))
            steps.wait()
            steps.inc(nc.vector.tensor_tensor(tmp_b[:, :], tmp_b[:, :], tmp_a[:, :], ALU.add))
            steps.wait()
            steps.inc(nc.vector.reciprocal(inv_1[:, :], tmp_b[:, :]))
            steps.inc(nc.vector.tensor_scalar(tmp_a[:, :], tmp_a[:, :], -1.0, 1.0, ALU.mult, ALU.add))
            steps.wait()
            steps.inc(nc.vector.tensor_tensor(inv_1[:, :], inv_1[:, :], tmp_a[:, :], ALU.mult))
            steps.wait()

            def moments(steps, src, tiles):
                for t in range(tiles):
                    last = nc.vector.bn_stats(stats[:, t, :], src[:, t, :])
                steps.inc(last)
                wait_apart(ve, steps.semaphore, steps.base + steps.n)
                for t in range(tiles):
                    last = nc.vector.bn_aggr(mv[:, t, :], stats[:, t, :])
                steps.inc(last)
                steps.wait()
                nc.vector.tensor_scalar(var_s[:, 0:tiles], mv[:, 0:tiles, 1], EPS, None, ALU.add).then_inc(var_ready, 1)

            post_base = 0
            for p in range(6):
                kind = KINDS[p]

                def transpose(k, u):
                    if u % 2 == 0:
                        ve.wait_ge(loaded[u // 2], LOADS_O + 16 * NA * (NCH * p + 1) + k * (16 * NA))
                    ve.wait_ge(mm_done, NU * NCH * p + k * NU + u + 1)
                    src = ring[:, u // 2, :].rearrange("p (g b q) -> p g b q", g=GR, q=Q)
                    src = src[:, :, u % 2 * SETS:(u % 2 + 1) * SETS, :]
                    dst = tring[:, u % TR].rearrange("p b (g q) -> p g b q", q=Q)
                    nc.vector.transpose(dst, src).then_inc(transposed, 1)

                def aggregate(k, parity):
                    if p not in AGG_DVE:
                        return
                    ve.wait_ge(xt_done, before(X_PASSES, p, 0) + 1)
                    cut = bass.ds(k * CH, CH)
                    if kind == "l1":
                        ve.wait_ge(agg_act, k + (NCH * p + 1))
                        ins = nc.vector.scalar_tensor_tensor(agg_s[:, :], xt[:, cut], om_a[:, :], agg_s[:, :],
                                                             ALU.mult, ALU.add)
                    else:
                        ve.wait_ge(mm_done, k * NU + (NU * (NCH * p + 1) + TR))
                        ve.wait_ge(y_ready, k + (NCH * p + 1))
                        ins = nc.vector.scalar_tensor_tensor(agg_s[:, :], psum[:, parity, :], 2.0, xt[:, cut],
                                                             ALU.mult, ALU.subtract)
                    ins.then_inc(agg_dve, 1)

                def ys_free(k):
                    wait_some(ve, xn_copied, before(LN_PASSES, p, k))
                    wait_some(ve, folded, before(FOLD_PASSES, p, k) * (16 * NA))
                    wait_some(ve, x_ready, before(X_PASSES, p, k))
                    if p == 5:
                        wait_some(ve, x3_stored, k * 16)

                def layernorm(k, p_index, src):
                    ve.wait_ge(rstd_ready, k + (p_index + 1))
                    for t in range(TPC):
                        last = nc.vector.tensor_scalar(ys[:, t, :], src[:, t, :], mv[:, t, 0:1], rstd[:, t:t + 1],
                                                       ALU.subtract, ALU.mult)
                    last.then_inc(ys_ready, 1)

                def epilogue(k, stage):
                    if stage == 0:
                        state[0] = Steps(ve, post, k * POST_STEPS[kind] + post_base)
                    steps = state[0]
                    chunk = bass.ds(k * TPC, TPC)
                    seen = k + (NCH * p + 2)
                    if stage == 0:
                        ve.wait_ge(y_ready, seen)
                        if kind == "in":
                            for t in range(TPC):
                                tile = bass.ds(k * TPC + t, 1)
                                last = nc.vector.scalar_tensor_tensor(
                                    rs[:, t, :], psum[:, 2, t * D:(t + 1) * D], inv_r[:, tile],
                                    row(res[:, tile, :]), ALU.mult, ALU.add)
                            last.then_inc(y_used, 1)
                            ve.wait_ge(y_used, seen)
                            moments(steps, rs, TPC)
                        elif kind == "l1":
                            for t in range(TPC):
                                tile = bass.ds(k * TPC + t, 1)
                                last = nc.vector.scalar_tensor_tensor(
                                    rs[:, t, :], psum[:, 2, t * D:(t + 1) * D], inv_1[:, tile], b1_s[:, :],
                                    ALU.mult, ALU.add)
                            last.then_inc(y_used, 1)
                            ve.wait_ge(y_used, seen)
                            steps.inc(nc.vector.scalar_tensor_tensor(rs[:, :, :], rs[:, :, :], 0.0,
                                                                     xn[:, chunk, :], ALU.max, ALU.add))
                            steps.wait()
                            moments(steps, rs, TPC)
                        elif kind == "cheb1":
                            ys_free(k)
                            nc.vector.tensor_copy(ys[:, :, :].rearrange("p t d -> p (t d)"), psum[:, 2, :])\
                              .then_inc(ys_ready, 1)
                            ve.wait_ge(ys_ready, k + (NCH * p + 1))
                            ve.sem_inc(y_used, 1)
                        else:
                            for t in range(TPC):
                                last = nc.vector.tensor_tensor(rs[:, t, :], psum[:, 2, t * D:(t + 1) * D],
                                                               b2_s[:, (p - 3) // 2, :], ALU.add)
                            last.then_inc(y_used, 1)
                            ve.wait_ge(y_used, seen)
                            if p == 5:
                                wait_some(ve, x_ready, before(X_PASSES, p, k))
                            nc.vector.tensor_scalar(ns[:, :, :], rs[:, :, :], 0.0, None, ALU.min).then_inc(elu_in, 1)
                            ve.wait_ge(elu_in, k + (before(ELU_PASSES, p, 0) + 1))
                            steps.inc(nc.vector.tensor_scalar(rs[:, :, :], rs[:, :, :], 0.0, None, ALU.max))
                    elif stage == 1:
                        if kind in ("in", "l1"):
                            ys_free(k)
                            layernorm(k, before(LN_PASSES, p, 0), rs)
                        elif kind == "cheb2":
                            ys_free(k)
                            steps.wait()
                            ve.wait_ge(elu_out, k + (before(ELU_PASSES, p, 0) + 1))
                            nc.vector.scalar_tensor_tensor(ys[:, :, :], ns[:, :, :], -1.0, rs[:, :, :],
                                                           ALU.add, ALU.add).then_inc(ys_ready, 1)
                        elif kind == "cheb2f":
                            steps.wait()
                            ve.wait_ge(elu_out, k + (before(ELU_PASSES, p, 0) + 1))
                            steps.inc(nc.vector.scalar_tensor_tensor(rs[:, :, :], ns[:, :, :], -1.0, rs[:, :, :],
                                                                     ALU.add, ALU.add))
                            steps.wait()
                            steps.inc(nc.vector.tensor_tensor(rs[:, :, :], rs[:, :, :], xn[:, chunk, :], ALU.add))
                            steps.wait()
                            moments(steps, rs, TPC)
                    elif stage == 2 and kind == "cheb2f":
                        ys_free(k)
                        layernorm(k, before(LN_PASSES, p, 0), rs)
                        ve.wait_ge(ys_ready, k + (NCH * p + 1))
                        for t in range(TPC):
                            last = nc.vector.tensor_tensor_reduce(out=rs[:, t, :], in0=ys[:, t, :], in1=ys[:, t, :],
                                                                  scale=1.0, scalar=0.0, op0=ALU.mult, op1=ALU.add,
                                                                  accum_out=ss[:, t:t + 1])
                        steps.inc(last)
                        steps.wait()
                        nc.vector.tensor_scalar(ss[:, :], ss[:, :], NORM_MIN2, None, ALU.max).then_inc(ss_ready, 1)
                    elif stage == 3:
                        if kind == "cheb2f":
                            ve.wait_ge(rn_ready, k + 1)
                            for t in range(TPC):
                                last = nc.vector.tensor_scalar(ns[:, t, :], ys[:, t, :], rn[:, t:t + 1], None, ALU.mult)
                            last.then_inc(ns_ready, 1)
                        assert steps.n == POST_STEPS[kind], (kind, steps.n)

                state = [None]

                def chunk(k, parity):
                    first = isinstance(k, int) and k == 0
                    for u in range(NU):
                        transpose(k, u)
                        if u == 1 and not first:
                            aggregate(k - 1, 1 - parity)
                        if 3 <= u <= 6 and not first:
                            epilogue(k - 1, u - 3)

                pairs(ve, chunk)
                aggregate(NCH - 1, 1)
                for stage in range(4):
                    epilogue(NCH - 1, stage)
                post_base += NCH * POST_STEPS[kind]

            ve.wait_ge(xn_copied, 3 * NCH)
            ve.wait_ge(x_ready, 4 * NCH)
            ve.wait_ge(xt_done, 4 * NCH + 1)
            h_base = 0
            for layer in range(2):
                R0 = NT * layer
                G0 = NT // 2 * layer

                def mask(g, tt, q):
                    ve.wait_ge(a_loaded[tt][q], g * 16 + 16 * (NT // 4 * layer + 1))
                    part = ring[:, tt, q * 2 * CH:(q + 1) * 2 * CH]
                    nc.vector.tensor_scalar(part, part, 0.0, NEG, ALU.is_le, ALU.mult).then_inc(masked, 1)

                def query_low(g, tt):
                    ve.wait_ge(qh_ready, g * 4 + (R0 + tt + 1))
                    nc.vector.tensor_tensor(q_l[:, tt % 2, :], q_f[:, 1, :], q_h[:, tt % 2, :].bitcast(fp32),
                                            ALU.subtract).then_inc(ql_ready, 1)

                def values_low(part):
                    ve.wait_ge(v_high, 2 * layer + part + 1)
                    half = slice(part * (NT // 2), (part + 1) * (NT // 2))
                    nc.vector.tensor_tensor(v_l[:, half, :], xn[:, half, :], v_h[:, half, :].bitcast(fp32),
                                            ALU.subtract).then_inc(v_split, 1)

                def finish_rows(g, tt):
                    G = g * 2 + (tt // 2 - 2)
                    steps = Steps(ve, h_done, G * H_STEPS[layer] + h_base)
                    wait_apart(ve, ot_ready, G + (G0 + 2))
                    steps.inc(nc.vector.tensor_reduce(out=rsum[:, :], in_=esum[:, bass.ds(G * 2, 2), :],
                                                      axis=AX.X, op=ALU.add))
                    steps.wait()
                    steps.inc(nc.vector.reciprocal(rsum[:, :], rsum[:, :]))
                    steps.wait()
                    for t in range(2):
                        last = nc.vector.tensor_scalar(hr[:, t, :], psum[:, 7, t * D:(t + 1) * D],
                                                       rsum[:, t:t + 1], None, ALU.mult)
                    last.then_inc(h_ready, 1)
                    ve.wait_ge(h_ready, G + (G0 + 1))
                    if layer == 0:
                        ve.wait_ge(hy_free, G + 1)
                        nc.vector.scalar_tensor_tensor(hy[:, :, :], hr[:, :, :], LEAK, hr[:, :, :],
                                                       ALU.mult, ALU.max).then_inc(hs_ready, 1)
                        ve.wait_ge(hs_ready, G + 1)
                        for t in range(2):
                            last = nc.vector.tensor_tensor_reduce(out=hr[:, t, :], in0=hy[:, t, :], in1=hy[:, t, :],
                                                                  scale=1.0, scalar=0.0, op0=ALU.mult, op1=ALU.add,
                                                                  accum_out=ss[:, t:t + 1])
                        steps.inc(last)
                        steps.wait()
                        nc.vector.tensor_scalar(ss[:, 0:2], ss[:, 0:2], NORM_MIN2, None, ALU.max)\
                          .then_inc(hss_ready, 1)
                    else:
                        steps.inc(nc.vector.scalar_tensor_tensor(hy[:, :, :], hr[:, :, :], LEAK, hr[:, :, :],
                                                                 ALU.mult, ALU.max))
                        steps.wait()
                        ve.wait_ge(x3_loaded, G * 16 + 16)
                        steps.inc(nc.vector.tensor_tensor(hy[:, :, :], hy[:, :, :], x3_s[:, :, :], ALU.add))
                        steps.wait()
                        moments(steps, hy, 2)
                    assert steps.n == H_STEPS[layer], steps.n

                def finish_norm(g, tt):
                    G = g * 2 + (tt // 2 - 2)
                    if layer == 0:
                        ve.wait_ge(hrn_ready, G + 1)
                        for t in range(2):
                            last = nc.vector.tensor_scalar(hz[:, t, :], hy[:, t, :], rn[:, t:t + 1], None, ALU.mult)
                        last.then_inc(hns_ready, 1)
                    else:
                        ve.wait_ge(rstd_ready, G + (3 * NCH + 1))
                        ve.wait_ge(out_free, G + 1)
                        for t in range(2):
                            last = nc.vector.tensor_scalar(hz[:, t, :], hy[:, t, :], mv[:, t, 0:1], rstd[:, t:t + 1],
                                                           ALU.subtract, ALU.mult)
                        last.then_inc(out_ready, 1)

                def step(g, tt, scores, back, ends):
                    more = scores and not (isinstance(g, int) and g * 4 + tt == NT - 1)
                    if scores:
                        ve.wait_ge(masked, g * 16 + 4 * (R0 + tt + 1))
                    for q in range(4):
                        if scores:
                            wait_apart(ve, s_ready, g * 16 + (4 * (R0 + tt) + q + 1))
                            b = 2 * (q % 2)
                            part = ring[:, tt, q * 2 * CH:(q + 1) * 2 * CH]
                            nc.vector.tensor_tensor_reduce(
                                out=part, in0=psum[:, b:b + 2, :].rearrange("p b c -> p (b c)"), in1=part,
                                scale=1.0, scalar=-3e38, op0=ALU.add, op1=ALU.max,
                                accum_out=mx[:, tt % 2, q:q + 1]).then_inc(s_masked, 1)
                        if scores and q == 3:
                            ve.wait_ge(s_masked, g * 16 + (4 * (R0 + tt) + 6))
                            nc.vector.tensor_reduce(out=nmx[:, tt:tt + 1], in_=mx[:, tt % 2, :], axis=AX.X,
                                                    op=ALU.max, negate=True).then_inc(max_ready, 1)
                        if back:
                            for w in (2 * q, 2 * q + 1):
                                ve.wait_ge(ev_high, g * 32 + (8 * (R0 + tt - 2) + w + 1))
                                cut = pt_cut(w, tt)
                                nc.vector.tensor_tensor(pt_l[cut], psum[:, 4 + w % 2, :].rearrange(
                                    "p (u i) -> p u i", i=P), pt_h[cut].bitcast(fp32), ALU.subtract)\
                                  .then_inc(ev_low, 1)
                        if more:
                            mask(*next_tile(g, tt), q)
                            if q == 1:
                                query_low(*next_tile(g, tt))
                        if ends and tt % 2 and q == 1:
                            finish_rows(g, tt)
                        if ends and tt % 2 and q == 2:
                            finish_norm(g, tt)
                    if isinstance(g, int) and g == 0 and tt < 2:
                        values_low(tt)

                for part in range(4):
                    cut = slice(part * (N // 4), (part + 1) * (N // 4))
                    ve.wait_ge(k_high, 4 * layer + part + 1)
                    nc.vector.tensor_tensor(k_l[:, cut], xt[:, cut], k_h[:, cut].bitcast(fp32), ALU.subtract)\
                      .then_inc(k_split, 1)
                query_low(0, 0)
                for q in range(4):
                    mask(0, 0, q)
                attention(ve, step)
                h_base += NT // 2 * H_STEPS[layer]

        @block.scalar
        def _(act):
            act.sem_inc(o_act, OT * FR)
            act.sem_inc(xt_done, 1)
            act.sem_inc(hk_ready, 1)
            act.dma_start(xn[:, :, :], x.rearrange("(t p) d -> p t d", p=P)).then_inc(x_in, 16)
            for a in range(NA):
                act.dma_start(xf[Q * a:Q * (a + 1), 0], x[RANGE * a:RANGE * (a + 1), :]
                              .rearrange("(b q) d -> q b d", q=Q)).then_inc(x_in, 16)
            act.dma_start(w_out_s[:, :], w_out).then_inc(consts, 16)
            act.dma_start(w_in_s[:, :], w_in).then_inc(consts, 16)
            act.dma_start(w1_s[:, :], w1t).then_inc(consts, 16)
            act.dma_start(w2_s[:, 0], w2a.rearrange("j d e -> d j e")).then_inc(consts, 16)
            act.dma_start(w2_s[:, 1], w2b.rearrange("j d e -> d j e")).then_inc(consts, 16)
            act.dma_start(b1_s[:, :], b1.partition_broadcast(P)).then_inc(consts, 16)
            act.dma_start(b2_s[:, 0], b2a.partition_broadcast(P)).then_inc(consts, 16)
            act.dma_start(b2_s[:, 1], b2b.partition_broadcast(P)).then_inc(consts, 16)
            act.dma_start(sc[:, 0:1], alpha.partition_broadcast(P)).then_inc(consts, 16)
            act.dma_start(sc[:, 1:2], beta1.partition_broadcast(P)).then_inc(consts, 16)
            act.dma_start(sc[:, 2:3], beta2.partition_broadcast(P)).then_inc(consts, 16)
            with act.Fori(0, 2) as sweep:
                for n in range(NO):
                    act.wait_ge(loaded[n % FR], sweep * (LOADS_O // 2) + 16 * (n // FR + 1))
                    tile = ring[:, n % FR, :].rearrange("p (t c) -> p t c", t=OT)
                    for t in range(OT):
                        act.wait_ge(o_act, sweep * (OT * NO) + (OT * (FR + n) + t))
                        nc.scalar.activation(junk, tile[:, t, :], ACT.Copy,
                                             accum_out=rowp[:, bass.ds(sweep, 1), n * OT + t:n * OT + t + 1]
                                             .rearrange("p a b -> p (a b)")).then_inc(o_act, 1)
                act.wait_ge(o_mm, sweep + 1)
                act.wait_ge(o_pe, sweep * NO + (NO + FR))
                nc.scalar.activation(out_s, psum[:, 0:4, :].rearrange("p b c -> p (b c)"), ACT.Copy)\
                  .then_inc(o_copied, 1)
                act.wait_ge(o_dve, sweep * NO + (NO + FR))
                nc.scalar.activation(col_s, psum[:, 4:8, :].rearrange("p b c -> p (b c)"), ACT.Copy)\
                  .then_inc(o_copied, 1)
            act.wait_ge(consts, 16 * N_CONSTS)

            for p in range(6):
                kind = KINDS[p]

                def stage(k, parity):
                    cut = bass.ds(k * CH, CH)
                    act.wait_ge(y_ready, k + (NCH * p + 1))
                    if kind in ("cheb2", "cheb2f"):
                        act.wait_ge(xt_done, before(X_PASSES, p, 0) + 1)
                        nc.scalar.activation(st0[:, :], xt[:, cut], ACT.Copy)
                        act.wait_ge(agg_act, NCH * p)
                        nc.scalar.activation(st1[:, :], t1t[:, cut], ACT.Copy).then_inc(agg_act, 1)
                        return
                    act.wait_ge(mm_done, k * NU + (NU * (NCH * p + 1) + TR))
                    if kind == "l1":
                        nc.scalar.activation(agg_s[:, :], psum[:, parity, :], ACT.Identity, scale=sc[:, 0:1])\
                          .then_inc(agg_act, 1)
                    elif kind == "in":
                        nc.scalar.activation(agg_s[:, :], psum[:, parity, :], ACT.Copy).then_inc(agg_act, 1)
                    else:
                        wait_some(act, agg_act, NCH * p)
                        nc.scalar.activation(t1t[:, cut], psum[:, parity, :], ACT.Copy)
                        nc.scalar.activation(agg_s[:, :], psum[:, parity, :], ACT.Copy).then_inc(agg_act, 1)

                def elu(k):
                    if p in ELU_PASSES:
                        act.wait_ge(elu_in, k + (before(ELU_PASSES, p, 0) + 1))
                        nc.scalar.activation(ns[:, :, :], ns[:, :, :], ACT.Exp).then_inc(elu_out, 1)

                def columns(k):
                    if p in X_PASSES:
                        wait_apart(act, x_ready, k + (before(X_PASSES, p, 0) + 1))
                        nc.scalar.activation(xt[:, bass.ds(k * CH, CH)], psum[:, 3, :], ACT.Copy).then_inc(xt_done, 1)

                def chunk(k, parity):
                    stage(k, parity)
                    if not (isinstance(k, int) and k == 0):
                        columns(k - 1)
                    elu(k)

                pairs(act, chunk)
                columns(NCH - 1)

            act.wait_ge(xt_done, 4 * NCH + 1)
            act.wait_ge(xn_copied, 3 * NCH)
            for layer in range(2):
                R0 = NT * layer
                G0 = NT // 2 * layer
                if layer == 1:
                    act.wait_ge(h_loaded[0], 16)
                for part in range(4):
                    cut = slice(part * (N // 4), (part + 1) * (N // 4))
                    nc.scalar.activation(k_h[:, cut], xt[:, cut], ACT.Copy).then_inc(k_high, 1)

                def query_high(g, tt):
                    act.wait_ge(q_made, g * 4 + (R0 + tt + 1))
                    nc.scalar.activation(q_h[:, tt % 2, :], q_f[:, 1, :], ACT.Copy).then_inc(qh_ready, 1)

                def step(g, tt, scores, back, ends):
                    more = scores and not (isinstance(g, int) and g * 4 + tt == NT - 1)
                    exp = (scores or tt == 0) and not (isinstance(g, int) and g * 4 + tt == 0)
                    G = g * 2 + (tt // 2 - 2)
                    for w in range(8):
                        if exp and w % 2 == 0:
                            q = w // 2
                            if q == 0:
                                act.wait_ge(max_ready, g * 4 + (R0 + tt))
                            slot = (tt - 1) % 4
                            part = ring[:, slot, q * 2 * CH:(q + 1) * 2 * CH]
                            nc.scalar.activation(part, part, ACT.Exp, bias=nmx[:, slot:slot + 1],
                                                 accum_out=row(esum[:, bass.ds(g * 4 + (tt - 1), 1), q:q + 1]))\
                              .then_inc(exp_done, 1)
                        if w == 2 and more:
                            query_high(*next_tile(g, tt))
                        if not back:
                            continue
                        if w == 0 and isinstance(g, int) and g == 0 and tt == 2:
                            act.wait_ge(v_split, 2 * (layer + 1))
                        act.wait_ge(tp_done, g * 32 + (8 * (R0 + tt - 2) + w + 1 + 8 * FR))
                        nc.scalar.activation(pt_h[pt_cut(w, tt)], psum[:, 4 + w % 2, :].rearrange(
                            "p (u i) -> p u i", i=P), ACT.Copy).then_inc(ev_high, 1)
                    if ends and tt % 2 == 0:
                        act.wait_ge(pv_done, G + (G0 + 1))
                        act.wait_ge(ot_ready, G + (G0 + 1))
                        nc.scalar.activation(o_s[:, :], psum[:, 6, 0:PT2], ACT.Copy).then_inc(o_staged, 1)
                    if ends and tt % 2 and layer == 0:
                        act.wait_ge(hk_free, G + 1)
                        act.wait_ge(hx_ready, G + 1)
                        nc.scalar.activation(hk[:, :], psum[:, 7, PT2:2 * PT2], ACT.Copy).then_inc(hk_ready, 1)

                query_high(0, 0)
                if layer == 1:
                    act.wait_ge(h_loaded[1], 16)
                for part in range(2):
                    half = slice(part * (NT // 2), (part + 1) * (NT // 2))
                    nc.scalar.activation(v_h[:, half, :], xn[:, half, :], ACT.Copy).then_inc(v_high, 1)
                attention(act, step)

        @block.gpsimd
        def _(pool):
            nc.gpsimd.memset(ones[:, :], 1.0).then_inc(ident_ready, 1)
            nc.gpsimd.memset(mhalf[:, :], -0.5).then_inc(ident_ready, 1)
            nc.gpsimd.memset(ident[:, :], 0.0).then_inc(ident_ready, 1)
            pool.wait_ge(ident_ready, 3)
            nc.gpsimd.affine_select(out=ident[:, :], in_=ident[:, :], compare_op=ALU.not_equal, fill=1.0,
                                    base=0, pattern=[[-1, P]], channel_multiplier=1).then_inc(ident_ready, 1)
            pool.sem_inc(hy_free, 1)
            pool.sem_inc(hk_free, 1)
            for p in range(6):
                for m in range(NCH // 2):
                    for kk in range(2):
                        if p in LN_PASSES:
                            pool.wait_ge(var_ready, m * 2 + (before(LN_PASSES, p, 0) + kk + 1))
                            nc.gpsimd.tensor_tensor(rstd[:, :], var_s[:, :], mhalf[:, :], ALU.pow)\
                              .then_inc(rstd_ready, 1)
                        pool.wait_ge(ys_ready, m * 2 + (NCH * p + kk + 1))
                        if p in FOLD_PASSES:
                            for s in range(NA):
                                b0 = NT // 2 * kk + s
                                dst = xf[Q * m:Q * (m + 1), (p + 1) % 2, b0:NT // 2 * kk + NT // 2:NA, :]
                                pool.dma_start(dst, ys[Q * s:Q * (s + 1), :, :]).then_inc(folded, 16)
                        if p == 5:
                            rows = (2 * m + kk) * CH
                            pool.dma_start(x3_d[rows:rows + CH, :].rearrange("(t p) d -> p t d", p=P), ys[:, :, :])\
                              .then_inc(x3_stored, 16)
                        if p in LN_PASSES:
                            nc.gpsimd.tensor_copy(xn[:, bass.ds(m * (2 * TPC) + kk * TPC, TPC), :], ys[:, :, :])\
                              .then_inc(xn_copied, 1)
                        if p == 5:
                            pool.wait_ge(ss_ready, m * 2 + (kk + 1))
                            nc.gpsimd.tensor_tensor(rn[:, :], ss[:, :], mhalf[:, :], ALU.pow).then_inc(rn_ready, 1)
            pool.wait_ge(x3_stored, 16 * NCH)
            for layer in range(2):
                R0 = NT * layer

                def query(g, tt):
                    if not (layer == 0 and isinstance(g, int) and g * 4 + tt == 0):
                        pool.wait_ge(ql_ready, g * 4 + (R0 + tt))
                    cut = bass.ds(g * (4 * P) + tt * P, P)
                    nc.gpsimd.tensor_tensor(q_f[:, 0, :], k_h[:, cut].bitcast(fp32), k_l[:, cut].bitcast(fp32),
                                            ALU.add).then_inc(q_raw, 1)
                    wait_apart(pool, q_raw, g * 4 + (R0 + tt + 1))
                    nc.gpsimd.tensor_scalar(q_f[:, 1, :], q_f[:, 0, :], sc[:, 1 + layer:2 + layer], None, ALU.mult)\
                      .then_inc(q_made, 1)

                def x3_rows(G):
                    return bass.ds(G * PT2, PT2)

                def step(g, tt, scores, back, ends):
                    G = g * 2 + (tt // 2 - 2)
                    if scores and not (isinstance(g, int) and g * 4 + tt == NT - 1):
                        query(*next_tile(g, tt))
                    if ends and tt % 2 and layer == 0:
                        wait_apart(pool, hs_ready, G + 1)
                        pool.dma_start(h_d[x3_rows(G), :].rearrange("(t p) d -> p t d", p=P), hy[:, :, :])\
                          .then_inc(h_stored, 16)
                        pool.wait_ge(hss_ready, G + 1)
                        nc.gpsimd.tensor_tensor(rn[:, 0:2], ss[:, 0:2], mhalf[:, 0:2], ALU.pow).then_inc(hrn_ready, 1)
                        wait_apart(pool, hk_ready, G + 2)
                        pool.dma_start(hk_d[:, x3_rows(G)], hk[:, :]).then_inc(hk_stored, 16)
                        pool.wait_ge(h_stored, G * 16 + 16)
                        pool.sem_inc(hy_free, 1)
                        pool.wait_ge(hk_stored, G * 16 + 16)
                        pool.sem_inc(hk_free, 1)
                    if ends and tt % 2 and layer == 1:
                        pool.wait_ge(var_ready, G + (3 * NCH + 1))
                        nc.gpsimd.tensor_tensor(rstd[:, 0:2], var_s[:, 0:2], mhalf[:, 0:2], ALU.pow)\
                          .then_inc(rstd_ready, 1)
                        wait_apart(pool, out_ready, G + 1)
                        pool.dma_start(out[x3_rows(G), :].rearrange("(t p) d -> p t d", p=P), hz[:, :, :])\
                          .then_inc(out_done, 16)
                        if not (isinstance(g, int) and g * 2 + tt // 2 - 2 == NT // 2 - 1):
                            pool.dma_start(x3_s[:, :, :], x3_d[x3_rows(G + 1), :].rearrange("(t p) d -> p t d", p=P))\
                              .then_inc(x3_loaded, 16)
                        pool.wait_ge(out_done, G * 16 + 16)
                        pool.sem_inc(out_free, 1)

                pool.wait_ge(k_split, 4 * (layer + 1))
                if layer == 1:
                    pool.sem_inc(out_free, 1)
                    pool.dma_start(x3_s[:, :, :], x3_d[0:PT2, :].rearrange("(t p) d -> p t d", p=P))\
                      .then_inc(x3_loaded, 16)
                query(0, 0)
                attention(pool, step)
            pool.wait_ge(out_done, 16 * (NT // 2))
    return nc


_INS = ["x", "adj", "L0_gnn_W_in", "L0_gnn_W_out", "L1_gnn_alpha", "L1_gnn_W", "L1_gnn_b",
        "L2_gnn_W0", "L2_gnn_b0", "L2_gnn_W1", "L2_gnn_b1", "L3_gnn_beta1", "L3_gnn_beta2"]


def kernel(**inputs):
    import numpy as np
    import concourse.bacc as bacc
    from concourse import mybir
    from concourse.bass_utils import run_bass_kernel_spmd

    nc = bacc.Bacc("TRN2", target_bir_lowering=False, num_devices=1)
    arrays, args = {}, []
    for name in _INS:
        a = np.asarray(inputs[name])
        if name == "L1_gnn_W":
            a = a.T
        a = np.ascontiguousarray(a)
        arrays[f"in_{name}_dram"] = a
        args.append(nc.dram_tensor(f"in_{name}_dram", a.shape, mybir.dt.from_np(a.dtype),
                                   kind="ExternalInput").ap())
    out = nc.dram_tensor("out_dram", (4096, 128), mybir.dt.float32, kind="ExternalOutput").ap()
    build_gnn_stack(nc, *args, out)
    r = run_bass_kernel_spmd(nc, [arrays], core_ids=[0])
    return r.results[0]["out_dram"]
```

```python
import concourse.bass as bass
from concourse import mybir
from contextlib import ExitStack


def build_gnn_stack(nc, x, adj, w_in, w_out, alpha, w1t, b1, w2a, b2a, w2b, b2b, beta1, beta2, out):
    fp32 = mybir.dt.float32
    fp32r = mybir.dt.float32r
    ALU = mybir.AluOpType
    ACT = mybir.ActivationFunctionType
    AX = mybir.AxisListType

    P = 128
    N, D = x.shape
    NT = N // P
    Q = 32
    NA = P // Q
    RANGE = N // NA
    CH = 512
    NCH = N // CH
    TPC = CH // P
    GR = CH // Q
    NU = 8
    QC = RANGE // NU
    SETS = QC // Q
    TILE = SETS * CH
    ORDER = (0, 2, 1, 4, 3, 6, 5, 7)
    LR = 4
    SR = 4
    HR = 2
    WR = 2
    FR = 4
    OC = N // 2
    OT = 2
    NO = NT // OT
    EPS = 1e-5
    NEG = -1e9
    LEAK = 0.3
    NORM_MIN2 = 1e-24

    KINDS = ["in", "l1", "cheb1", "cheb2", "cheb1", "cheb2f"]
    RES_PASSES = [1, 5]
    AGG_DVE = [1, 3, 5]
    X_PASSES = [0, 1, 3, 5]
    LN_PASSES = [0, 1, 5]
    ELU_PASSES = [3, 5]
    FOLD_PASSES = [0, 1, 2, 3, 4]

    def nth(passes, p, k):
        return NCH * passes.index(p) + k

    ctx = ExitStack()
    with ctx:
        def sb(name, shape, dt=fp32):
            return ctx.enter_context(nc.sbuf_tensor(name, shape, dt))

        def sem(name):
            return ctx.enter_context(nc.semaphore(name))

        sc = sb("sc", [P, 3])
        ident = sb("ident", [P, P])
        mhalf = sb("mhalf", [P, TPC])
        stats = sb("stats", [P, TPC, 6])
        mv = sb("mv", [P, TPC, 2])
        var_s = sb("var_s", [P, TPC])
        rstd = sb("rstd", [P, TPC])
        ss = sb("ss", [P, TPC])
        rn = sb("rn", [P, TPC])
        with nc.sbuf_tensor("ring", [P, FR, N], fp32) as ring:
            pass
        load_ring = sb("load_ring", [P, LR, TILE])
        high_ring = sb("high_ring", [P, HR, SETS, CH], fp32r)
        whole_ring = sb("whole_ring", [P, WR, SETS, CH])

        with ExitStack() as passes_ctx:
            def sb_a(name, shape, dt=fp32):
                return passes_ctx.enter_context(nc.sbuf_tensor(name, shape, dt))

            xt = sb_a("xt", [P, N])
            t1t = sb_a("t1t", [P, N])
            with nc.sbuf_tensor("tring", [P, SR, SETS, CH], fp32) as tring:
                pass
            low_ring = sb_a("low_ring", [P, SR, SETS, CH], fp32r)
            with nc.sbuf_tensor("x_first", [P, 2, NT, D], fp32) as x_first:
                pass
            xp = sb_a("xp", [P, 2, 2, NA, 2, 2, D], fp32r)
            xw = sb_a("xw", [P, 2, 2, NA, 2, D])
            agg_s = sb_a("agg_s", [P, CH])
            st0 = sb_a("st0", [P, CH])
            st1 = sb_a("st1", [P, CH])
            rs = sb_a("rs", [P, TPC, D])
            ys = sb_a("ys", [P, TPC, D])
            yp = sb_a("yp", [P, 2, 2, D], fp32r)
            xr = sb_a("xr", [P, 2, TPC, D])
            ns = sb_a("ns", [P, TPC, D])
            w_in_s = sb_a("w_in_s", [P, D])
            w_out_s = sb_a("w_out_s", [P, D])
            w1_s = sb_a("w1_s", [P, D])
            w2_s = sb_a("w2_s", [P, 2, 3, D])
            b1_s = sb_a("b1_s", [P, D])
            b2_s = sb_a("b2_s", [P, 2, D])
            om_a = sb_a("om_a", [P, 1])
            ones = sb_a("ones", [P, 1])
            rowp = sb_a("rowp", [P, 2, NT])
            inv_r = sb_a("inv_r", [P, NT])
            inv_1 = sb_a("inv_1", [P, NT])
            tmp_a = sb_a("tmp_a", [P, NT])
            tmp_b = sb_a("tmp_b", [P, NT])
            inv_c = sb_a("inv_c", [P, NT // 2])

        PT2 = 2 * P
        pt_h = sb("pt_h", [P, NT, PT2], fp32r)
        pt_l = sb("pt_l", [P, NT, PT2], fp32r)
        k_h = sb("k_h", [P, N], fp32r)
        k_l = sb("k_l", [P, N], fp32r)
        v_h = sb("v_h", [P, NT, D], fp32r)
        v_l = sb("v_l", [P, NT, D], fp32r)
        o_s = sb("o_s", [P, PT2])
        hr = sb("hr", [P, 2, D])
        hy = sb("hy", [P, 2, D])
        hz = sb("hz", [P, 2, D])
        hk = sb("hk", [P, PT2])
        x3_s = sb("x3_s", [P, 2, D])
        q_f = sb("q_f", [P, 2, P])
        q_h = sb("q_h", [P, 2, P], fp32r)
        q_l = sb("q_l", [P, 2, P], fp32r)
        mx = sb("mx", [P, 2, 4])
        nmx = sb("nmx", [P, 4])
        esum = sb("esum", [P, NT, 4])
        rsum = sb("rsum", [P, 2])

        x1_d = nc.dram_tensor("x1_d", [N, D], fp32, kind="Internal").ap()
        x2_d = nc.dram_tensor("x2_d", [N, D], fp32, kind="Internal").ap()
        x3_d = nc.dram_tensor("x3_d", [N, D], fp32, kind="Internal").ap()
        h_d = nc.dram_tensor("h_d", [N, D], fp32, kind="Internal").ap()
        hk_d = nc.dram_tensor("hk_d", [P, N], fp32, kind="Internal").ap()
        psum = ctx.enter_context(nc.psum_tensor("psum", [P, 8, CH], fp32))

        tflat = tring[:, :, :, :].rearrange("p a b c -> p (a b c)")
        out_s = tflat[:, 2 * OC:3 * OC]
        col_s = tflat[:, 3 * OC:4 * OC]
        junk = xw[:, 1].rearrange("p k s j d -> p (k s j d)")
        res = t1t[:, :].rearrange("p (t d) -> p t d", d=D)
        x0 = xt[:, :].rearrange("p (t d) -> p t d", d=D)
        xn = res
        x_folded = x_first[:, 1]

        def split_tile(u):
            return tring[:, u // 2 % SR]

        def low_tile(u):
            return low_ring[:, u // 2 % SR]

        def high_tile(u):
            return high_ring[:, u // 2 % HR]

        def whole_tile(u):
            return whole_ring[:, u // 2 % WR]

        loaded = [sem(f"loaded{i}") for i in range(FR)]
        tile_in = [sem(f"tile_in{i}") for i in range(LR)]
        consts = sem("consts")
        carried = sem("carried")
        x0_in = [sem("x0_in0"), sem("x0_in1")]
        x_in = sem("x_in")
        ident_ready = sem("ident_ready")
        o_pe = sem("o_pe")
        o_act = sem("o_act")
        o_dve = sem("o_dve")
        o_copied = sem("o_copied")
        o_mm = sem("o_mm")
        o_scale = sem("o_scale")
        o_res = sem("o_res")
        dve_step = sem("dve_step")
        transposed = sem("transposed")
        high_made = sem("high_made")
        low_made = sem("low_made")
        mm_done = sem("mm_done")
        x_high = sem("x_high")
        x_split = sem("x_split")
        x_whole = sem("x_whole")
        xr_in = [sem("xr_in0"), sem("xr_in1")]
        xr_used = sem("xr_used")
        ys_high = sem("ys_high")
        ys_split = sem("ys_split")
        x_stored = sem("x_stored")
        agg_act = sem("agg_act")
        agg_dve = sem("agg_dve")
        y_ready = sem("y_ready")
        y_used = sem("y_used")
        post = sem("post")
        elu_in = sem("elu_in")
        elu_out = sem("elu_out")
        var_ready = sem("var_ready")
        rstd_ready = sem("rstd_ready")
        ss_ready = sem("ss_ready")
        rn_ready = sem("rn_ready")
        ys_ready = sem("ys_ready")
        ns_ready = sem("ns_ready")
        xn_copied = sem("xn_copied")
        folded = [sem("folded_even"), sem("folded_odd")]
        folded_whole = [sem("whole_even"), sem("whole_odd")]
        x_ready = sem("x_ready")
        xt_done = sem("xt_done")
        s_ready = sem("s_ready")
        s_masked = sem("s_masked")
        a_loaded = [[sem(f"a_loaded{i}_{q}") for q in range(4)] for i in range(FR)]
        masked = sem("masked")
        max_ready = sem("max_ready")
        exp_done = sem("exp_done")
        tp_done = sem("tp_done")
        ev_high = sem("ev_high")
        ev_low = sem("ev_low")
        k_high = sem("k_high")
        k_split = sem("k_split")
        v_high = sem("v_high")
        v_split = sem("v_split")
        q_raw = sem("q_raw")
        q_made = sem("q_made")
        qh_ready = sem("qh_ready")
        ql_ready = sem("ql_ready")
        pv_done = sem("pv_done")
        o_staged = sem("o_staged")
        ot_ready = sem("ot_ready")
        h_done = sem("h_done")
        h_ready = sem("h_ready")
        hs_ready = sem("hs_ready")
        hss_ready = sem("hss_ready")
        hrn_ready = sem("hrn_ready")
        h_stored = sem("h_stored")
        hy_free = sem("hy_free")
        hns_ready = sem("hns_ready")
        hx_ready = sem("hx_ready")
        hk_ready = sem("hk_ready")
        hk_stored = sem("hk_stored")
        hk_free = sem("hk_free")
        x3_loaded = sem("x3_loaded")
        hk_loaded = [sem(f"hk_loaded{i}") for i in range(4)]
        hv_loaded = sem("hv_loaded")
        out_ready = sem("out_ready")
        out_done = sem("out_done")
        out_free = sem("out_free")

        def pairs(eng, body):
            body(0, 0)
            body(1, 1)
            with eng.Fori(1, NCH // 2) as m:
                body(m * 2, 0)
                body(m * 2 + 1, 1)

        def before(passes, p, k):
            whole = NCH * len([q for q in passes if q < p])
            return whole + k if p in passes else whole

        def wait_apart(eng, semaphore, value):
            eng.wait_ge(semaphore, value)
            eng.sem_inc(carried, 1)

        def wait_some(eng, semaphore, value):
            if not (isinstance(value, int) and value <= 0):
                eng.wait_ge(semaphore, value)

        def attention(eng, step):
            for g in range(2):
                for tt in range(4):
                    step(g, tt, True, g > 0 or tt >= 2, g > 0)
            with eng.Fori(2, NT // 4 - 1) as g:
                for tt in range(4):
                    step(g, tt, True, True, True)
            for tt in range(4):
                step(NT // 4 - 1, tt, True, True, True)
            for tt in range(4):
                step(NT // 4, tt, False, tt < 2, True)

        def normed(g, tt, ends):
            if not ends or tt % 2 and not (isinstance(g, int) and g * 4 + tt == NT + 3):
                return None
            if isinstance(g, int) and g * 4 + tt == 4:
                return None
            return g * 2 + (tt // 2 - 2 - (tt % 2 == 0))

        def next_tile(g, tt):
            return (g, tt + 1) if tt < 3 else (g + 1, 0)

        def pt_cut(w, tt):
            return (slice(None), slice(4 * w, 4 * w + 4), slice(tt % 2 * P, (tt % 2 + 1) * P))

        def row(ap):
            return ap.rearrange("p a d -> p (a d)")

        class Steps:

            def __init__(self, eng, semaphore, base):
                self.eng, self.semaphore, self.base, self.n = eng, semaphore, base, 0

            def inc(self, instruction):
                instruction.then_inc(self.semaphore, 1)
                self.n += 1

            def wait(self):
                self.eng.wait_ge(self.semaphore, self.base + self.n)

        block = ctx.enter_context(nc.Block())

        @block.sync
        def _(sp):
            first = FR * OT
            rows = x.rearrange("(t p) d -> p t d", p=P)
            sp.dma_start(x0[:, 0:first, :], rows[:, 0:first, :]).then_inc(x0_in[0], 16)
            for sweep in range(2):
                for n in range(NO):
                    if sweep == 0 and n == 1:
                        sp.dma_start(x0[:, first:NT, :], rows[:, first:NT, :]).then_inc(x0_in[1], 16)
                    sp.wait_ge(o_pe, sweep * NO + n + 1)
                    sp.wait_ge(o_act, sweep * (OT * NO) + OT * (n + 1))
                    sp.wait_ge(o_dve, sweep * NO + n + 1)
                    src = adj[n * OT * P:(n + 1) * OT * P, sweep * OC:(sweep + 1) * OC]
                    sp.dma_start(ring[:, n % FR, :].rearrange("p (t c) -> p t c", t=OT),
                                 src.rearrange("(t p) c -> p t c", p=P)).then_inc(loaded[n % FR], 16)
            done = 2 * NO + FR - FR // 2
            sp.wait_ge(o_pe, done)
            sp.wait_ge(o_act, OT * done)
            sp.wait_ge(o_dve, done)
            for p in range(6):
                with sp.Fori(0, NCH // 2) as m:
                    for kk in range(2):
                        for i in range(NU):
                            wait_apart(sp, transposed, m * (2 * NU) + (NU * (NCH * p + kk) + i + 1))
                            for a in range(NA):
                                c0 = RANGE * a + QC * ORDER[i]
                                src = adj[bass.ds(m * (2 * CH) + kk * CH, CH), c0:c0 + QC]
                                dst = load_ring[Q * a:Q * (a + 1), i % LR, :].rearrange("p (g c) -> p g c", c=QC)
                                sp.dma_start(dst, src.rearrange("(g q) c -> q g c", q=Q))\
                                  .then_inc(tile_in[i % LR], 16)
                        if p in RES_PASSES:
                            sp.wait_ge(x_stored, 16 * NCH * (RES_PASSES.index(p) + 1))
                            wait_apart(sp, xr_used, m * 2 + (nth(RES_PASSES, p, kk) + 1))
                            x_d = x1_d if p == 1 else x2_d
                            sp.dma_start(xr[:, kk], x_d[bass.ds(m * (2 * CH) + kk * CH, CH), :]
                                         .rearrange("(t p) d -> p t d", p=P)).then_inc(xr_in[kk], 16)
            sp.wait_ge(mm_done, NU * NCH * 6 + NU)
            for layer in range(2):
                def tile_rows(g, tt):
                    for q in range(4):
                        wait_apart(sp, tp_done, g * 32 + (8 * NT * layer + 8 * tt + 2 * q + 2))
                        cut = slice(q * 2 * CH, (q + 1) * 2 * CH)
                        sp.dma_start(ring[:, tt, cut], adj[bass.ds(g * 4 * P + tt * P, P), cut])\
                          .then_inc(a_loaded[tt][q], 16)

                tile_rows(0, 0)
                tile_rows(0, 1)
                if layer == 1:
                    sp.wait_ge(pv_done, NT // 2)
                    sp.wait_ge(hk_stored, 16 * (NT // 2))
                    for part in range(4):
                        cut = slice(part * (N // 4), (part + 1) * (N // 4))
                        sp.dma_start(xt[:, cut], hk_d[:, cut]).then_inc(hk_loaded[part], 16)
                    sp.wait_ge(h_stored, 16 * (NT // 2))
                    sp.dma_start(xn[:, :, :], h_d.rearrange("(t p) d -> p t d", p=P)).then_inc(hv_loaded, 16)
                tile_rows(0, 2)
                tile_rows(0, 3)
                with sp.Fori(1, NT // 4) as g:
                    for tt in range(4):
                        tile_rows(g, tt)

        N_CONSTS = 11
        LOADS_O = 2 * NO // FR * 16

        @block.tensor
        def _(pe):
            pe.sem_inc(o_pe, FR)
            pe.sem_inc(mm_done, NU)
            pe.sem_inc(y_ready, 1)
            pe.sem_inc(o_mm, 1)
            pe.sem_inc(ot_ready, 1)
            pe.sem_inc(tp_done, 8 * FR)
            pe.wait_ge(x0_in[0], 16)
            with pe.Fori(0, 2) as sweep:
                for n in range(NO):
                    if n == FR:
                        pe.wait_ge(x0_in[1], 16)
                    pe.wait_ge(loaded[n % FR], sweep * (LOADS_O // 2) + 16 * (n // FR + 1))
                    tile = ring[:, n % FR, :].rearrange("p (t c) -> p t c", t=OT)
                    for t in range(OT):
                        for c in range(OC // CH):
                            last = nc.tensor.matmul(psum[:, c, :], x0[:, n * OT + t, :],
                                                    tile[:, t, c * CH:(c + 1) * CH],
                                                    start=(n + t == 0), stop=(n == NO - 1 and t == OT - 1))
                    last.then_inc(o_pe, 1)
                pe.wait_ge(ident_ready, 4)
                pe.wait_ge(consts, 16 * N_CONSTS)
                pe.wait_ge(o_copied, sweep * 5 + 1)
                for t in range(NT // 2):
                    last = nc.tensor.matmul(psum[:, 4, t:t + 1], col_s[:, t * P:(t + 1) * P], ones[:, :],
                                            start=True, stop=True)
                last.then_inc(o_mm, 1)
                pe.wait_ge(o_scale, sweep + 1)
                for bank in range(4):
                    pe.wait_ge(o_copied, sweep * 5 + bank + 2)
                    for t in range(TPC):
                        cut = slice((bank * TPC + t) * P, (bank * TPC + t + 1) * P)
                        last = nc.tensor.matmul(psum[:, 4 + bank, t * D:(t + 1) * D], out_s[:, cut], w_out_s[:, :],
                                                start=True, stop=True)
                    last.then_inc(o_mm, 1)
            pe.wait_ge(x_split, 4)
            pe.wait_ge(x_whole, 16 * 4 * NA)

            def multiply(p, k, parity, u):
                kk, t = divmod(u, TPC)
                if u % 2 == 0:
                    pe.wait_ge(low_made, k * (NU // 2) + (NU // 2 * NCH * p + u // 2 + 1))
                    high, low = high_tile(u), low_tile(u)
                else:
                    pe.wait_ge(transposed, k * NU + (NU * NCH * p + ORDER.index(u) + 1 + LR))
                    whole = whole_tile(u)
                for s in range(SETS):
                    start, stop = u + s == 0, (u == NU - 1 and s == SETS - 1)
                    if u % 2 == 0:
                        x_high_part, x_low_part = (xp[:, p % 2, kk, s, t // 2, i, :] for i in range(2))
                        nc.tensor.matmul(psum[:, parity, :], x_high_part, high[:, s, :], start=start, stop=stop)
                        nc.tensor.matmul(psum[:, parity, :], x_high_part, low[:, s, :], start=False, stop=stop)
                        last = nc.tensor.matmul(psum[:, parity, :], x_low_part, high[:, s, :],
                                                start=False, stop=stop)
                    else:
                        last = nc.tensor.matmul(psum[:, parity, :], xw[:, p % 2, kk, s, t // 2, :],
                                                whole[:, s, :], start=start, stop=stop)
                last.then_inc(mm_done, 1)

            def pass_steps(p):
                kind = KINDS[p]

                def rows(k):
                    pe.wait_ge(agg_act, NCH * p + k + 1)
                    if p in AGG_DVE:
                        pe.wait_ge(agg_dve, nth(AGG_DVE, p, 0) + k + 1)
                    pe.wait_ge(y_used, NCH * p + k + 1)
                    for t in range(TPC):
                        o = psum[:, 2, t * D:(t + 1) * D]
                        cut = slice(t * P, (t + 1) * P)
                        if kind == "in":
                            last = nc.tensor.matmul(o, agg_s[:, cut], w_in_s[:, :], start=True, stop=True)
                        elif kind == "l1":
                            last = nc.tensor.matmul(o, agg_s[:, cut], w1_s[:, :], start=True, stop=True)
                        elif kind == "cheb1":
                            last = nc.tensor.transpose(o, agg_s[:, cut], ident[:, :])
                        else:
                            w = w2_s[:, (p - 3) // 2]
                            nc.tensor.matmul(o, st0[:, cut], w[:, 0, :], start=True, stop=False)
                            nc.tensor.matmul(o, st1[:, cut], w[:, 1, :], start=False, stop=False)
                            last = nc.tensor.matmul(o, agg_s[:, cut], w[:, 2, :], start=False, stop=True)
                    last.then_inc(y_ready, 1)

                def columns(k):
                    if p not in X_PASSES:
                        return
                    if p == 5:
                        pe.wait_ge(ns_ready, k + 1)
                    else:
                        pe.wait_ge(ys_ready, NCH * p + k + 1)
                    pe.wait_ge(xt_done, before(X_PASSES, p, k) + 1)
                    for t in range(TPC):
                        src = ns[:, t, :] if p == 5 else ys[:, t, :]
                        last = nc.tensor.transpose(psum[:, 3, t * P:(t + 1) * P], src, ident[:, :])
                    last.then_inc(x_ready, 1)

                return rows, columns

            rows, columns = None, None
            for p in range(6):
                last_rows, last_columns = rows, columns
                rows, columns = pass_steps(p)

                def chunk(k, parity):
                    first = isinstance(k, int) and k == 0
                    for u in range(NU):
                        if first and p > 0 and u % TPC == 0:
                            pe.wait_ge(folded[u // TPC], NA * 16 * (NCH // 2) * p)
                            pe.wait_ge(folded_whole[u // TPC], NA * 16 * (NCH // 2) * p)
                        multiply(p, k, parity, u)
                        if u == 1 and p == 5 and not (isinstance(k, int) and k < 2):
                            columns(k - 2)
                        if u == 1 and not first:
                            rows(k - 1)
                        if u == 0 and first and p > 0:
                            last_rows(NCH - 1)
                        if u == TPC - 1 and first and p > 0:
                            last_columns(NCH - 1)
                    if not first and p < 5:
                        columns(k - 1)

                pairs(pe, chunk)
            columns(NCH - 2)
            rows(NCH - 1)
            columns(NCH - 1)

            for layer in range(2):
                R0 = NT * layer
                G0 = NT // 2 * layer

                BLOCKS = ({1: 4, 3: 5, 5: 6, 7: 7}, {2: 0, 4: 1, 6: 2, 7: 3})

                def product(block):
                    for u in range(4 * block, 4 * block + 4):
                        for v, probs in ((v_h, pt_h), (v_h, pt_l), (v_l, pt_h)):
                            last = nc.tensor.matmul(psum[:, 6, 0:PT2], v[:, u, :], probs[:, u, :],
                                                    start=(u == 0 and v is v_h and probs is pt_h),
                                                    stop=(u == NT - 1 and v is v_l))
                    if block == 7:
                        last.then_inc(pv_done, 1)

                def step(g, tt, scores, back, ends):
                    if scores:
                        pe.wait_ge(ql_ready, g * 4 + (R0 + tt + 1))
                    for q in range(4):
                        if isinstance(g, int) and g * 4 + tt == 0:
                            pe.wait_ge(k_split, 4 * layer + q + 1)
                        if scores:
                            pe.wait_ge(s_masked, g * 16 + (4 * (R0 + tt) + q + 1))
                            slot = tt % 2
                            for weights, parts in ((q_h, (k_h, k_l)), (q_l, (k_h,))):
                                for c in range(2):
                                    j = (2 * q + c) * CH
                                    for part in parts:
                                        last = nc.tensor.matmul(psum[:, 2 * (q % 2) + c, :], weights[:, slot, :],
                                                                part[:, j:j + CH],
                                                                start=(weights is q_h and part is k_h),
                                                                stop=(weights is q_l), skip_group_check=True)
                            last.then_inc(s_ready, 1)
                        if back and q == 0:
                            pe.wait_ge(exp_done, g * 16 + 4 * (R0 + tt - 1))
                        for w in (2 * q, 2 * q + 1):
                            if w in BLOCKS[tt % 2] and (ends if tt % 2 == 0 else back):
                                block = BLOCKS[tt % 2][w]
                                if block == 0 and isinstance(g, int) and g == 0:
                                    pe.wait_ge(v_split, 2 * (layer + 1))
                                tile_2 = R0 + tt - (2 if tt % 2 else 3)
                                pe.wait_ge(ev_low, g * 32 + (8 * tile_2 + block + 1 + 2))
                                product(block)
                            if back:
                                pe.wait_ge(ev_low, g * 32 + (8 * (R0 + tt - 2) + w + 1))
                                for i in range(4):
                                    u = 4 * w + i
                                    last = nc.tensor.transpose(psum[:, 4 + w % 2, i * P:(i + 1) * P],
                                                               ring[:, (tt - 2) % 4, u * P:(u + 1) * P], ident[:, :])
                                last.then_inc(tp_done, 1)
                            if ends and tt % 2 and w == 1:
                                G = g * 2 + (tt // 2 - 2)
                                pe.wait_ge(o_staged, G + (G0 + 1))
                                if layer == 0:
                                    pe.wait_ge(hk_ready, G + 1)
                                else:
                                    pe.wait_ge(h_ready, G + G0)
                                for t in range(2):
                                    last = nc.tensor.transpose(psum[:, 7, t * P:(t + 1) * P],
                                                               o_s[:, t * P:(t + 1) * P], ident[:, :])
                                last.then_inc(ot_ready, 1)
                    G = normed(g, tt, ends)
                    if G is not None and layer == 0:
                        pe.wait_ge(hns_ready, G + 1)
                        for t in range(2):
                            last = nc.tensor.transpose(psum[:, 7, PT2 + t * P:PT2 + (t + 1) * P],
                                                       hz[:, t, :], ident[:, :])
                        last.then_inc(hx_ready, 1)

                attention(pe, step)

        SWEEP_STEPS = NO * OT + 4
        POST_STEPS = {"in": 2, "l1": 3, "cheb1": 0, "cheb2": 1, "cheb2f": 6}
        H_STEPS = (3, 6)

        @block.vector
        def _(ve):
            ve.sem_inc(o_dve, FR)
            ve.sem_inc(o_res, 1)
            ve.sem_inc(transposed, LR)
            ve.sem_inc(xr_used, 2)
            ve.sem_inc(y_used, 1)
            ve.sem_inc(s_masked, 2)
            ve.sem_inc(ev_low, 2)
            deg_c = psum[:, 4, 0:NT // 2]

            def transpose(p, k, i):
                u = ORDER[i]
                ve.wait_ge(tile_in[i % LR], k * (32 * NA) + 16 * NA * (2 * NCH * p + i // LR + 1))
                back = NU if u % 2 == 0 else 2 * WR
                ve.wait_ge(mm_done, k * NU + (NU * NCH * p + u + 1 - back + NU))
                dst = split_tile(u) if u % 2 == 0 else whole_tile(u)
                src = load_ring[:, i % LR, :].rearrange("p (g b q) -> p g b q", g=GR, q=Q)
                nc.vector.transpose(dst.rearrange("p b (g q) -> p g b q", q=Q), src).then_inc(transposed, 1)

            for sweep in range(2):
                steps = Steps(ve, dve_step, sweep * SWEEP_STEPS)
                ve.wait_ge(o_res, sweep + 1)
                acc = psum[:, 4:8, :].rearrange("p b c -> p (b c)")
                for n in range(NO):
                    ve.wait_ge(loaded[n % FR], sweep * (LOADS_O // 2) + 16 * (n // FR + 1))
                    tile = ring[:, n % FR, :].rearrange("p (t c) -> p t c", t=OT)
                    for t in range(OT):
                        if n + t == 0:
                            ins = nc.vector.tensor_copy(acc, tile[:, t, :])
                        else:
                            steps.wait()
                            ins = nc.vector.tensor_tensor(acc, acc, tile[:, t, :], ALU.add)
                        steps.inc(ins)
                    steps.wait()
                    ve.sem_inc(o_dve, 1)
                if sweep == 1:
                    transpose(0, 0, 0)
                    transpose(0, 0, 1)
                ve.wait_ge(o_mm, sweep * 5 + 2)
                half = slice(0, NT // 2)
                steps.inc(nc.vector.tensor_scalar(tmp_a[:, half], deg_c, 0.0, None, ALU.is_gt))
                steps.wait()
                steps.inc(nc.vector.tensor_tensor(tmp_b[:, half], deg_c, tmp_a[:, half], ALU.mult))
                steps.wait()
                steps.inc(nc.vector.scalar_tensor_tensor(tmp_b[:, half], tmp_b[:, half], 1.0, tmp_a[:, half],
                                                         ALU.add, ALU.subtract))
                steps.wait()
                steps.inc(nc.vector.reciprocal(inv_c[:, :], tmp_b[:, half]))
                steps.wait()
                ve.sem_inc(o_scale, 1)
                ve.wait_ge(x0_in[1], 16)
                for t in range(NT // 2):
                    if t % TPC == 0:
                        ve.wait_ge(o_mm, sweep * 5 + (t // TPC + 3))
                    node_tile = slice(sweep * (NT // 2) + t, sweep * (NT // 2) + t + 1)
                    last = nc.vector.scalar_tensor_tensor(
                        row(res[:, node_tile, :]), psum[:, 4 + t // TPC, t % TPC * D:(t % TPC + 1) * D],
                        inv_c[:, t:t + 1], row(x0[:, node_tile, :]), ALU.mult, ALU.add)
                last.then_inc(o_res, 1)

            def row_scales():
                steps = Steps(ve, dve_step, 2 * SWEEP_STEPS)
                ve.wait_ge(o_act, OT * (2 * NO + FR))
                ve.wait_ge(consts, 16 * N_CONSTS)
                deg = rowp[:, 0, :]
                steps.inc(nc.vector.tensor_tensor(deg, rowp[:, 0, :], rowp[:, 1, :], ALU.add))
                steps.inc(nc.vector.tensor_scalar(om_a[:, :], sc[:, 0:1], -1.0, 1.0, ALU.mult, ALU.add))
                steps.wait()
                steps.inc(nc.vector.tensor_scalar(tmp_a[:, :], deg, 0.0, None, ALU.is_gt))
                steps.wait()
                steps.inc(nc.vector.tensor_tensor(tmp_b[:, :], deg, tmp_a[:, :], ALU.mult))
                steps.wait()
                steps.inc(nc.vector.scalar_tensor_tensor(tmp_b[:, :], tmp_b[:, :], 1.0, tmp_a[:, :],
                                                         ALU.add, ALU.subtract))
                steps.wait()
                steps.inc(nc.vector.reciprocal(inv_r[:, :], tmp_b[:, :]))
                steps.wait()
                steps.inc(nc.vector.tensor_scalar(tmp_b[:, :], deg, sc[:, 0:1], om_a[:, :], ALU.mult, ALU.add))
                steps.wait()
                steps.inc(nc.vector.tensor_scalar(tmp_a[:, :], tmp_b[:, :], 0.0, None, ALU.is_equal))
                steps.wait()
                steps.inc(nc.vector.tensor_tensor(tmp_b[:, :], tmp_b[:, :], tmp_a[:, :], ALU.add))
                steps.wait()
                steps.inc(nc.vector.reciprocal(inv_1[:, :], tmp_b[:, :]))
                steps.inc(nc.vector.tensor_scalar(tmp_a[:, :], tmp_a[:, :], -1.0, 1.0, ALU.mult, ALU.add))
                steps.wait()
                steps.inc(nc.vector.tensor_tensor(inv_1[:, :], inv_1[:, :], tmp_a[:, :], ALU.mult))
                steps.wait()

            def moments(steps, src, tiles):
                for t in range(tiles):
                    last = nc.vector.bn_stats(stats[:, t, :], src[:, t, :])
                steps.inc(last)
                wait_apart(ve, steps.semaphore, steps.base + steps.n)
                for t in range(tiles):
                    last = nc.vector.bn_aggr(mv[:, t, :], stats[:, t, :])
                steps.inc(last)
                steps.wait()
                nc.vector.tensor_scalar(var_s[:, 0:tiles], mv[:, 0:tiles, 1], EPS, None, ALU.add).then_inc(var_ready, 1)

            def pass_steps(p, post_base):
                kind = KINDS[p]

                def aggregate(k, parity):
                    if p not in AGG_DVE:
                        return
                    ve.wait_ge(xt_done, before(X_PASSES, p, 0) + 1)
                    cut = bass.ds(k * CH, CH)
                    if kind == "l1":
                        ve.wait_ge(agg_act, k + (NCH * p + 1))
                        ins = nc.vector.scalar_tensor_tensor(agg_s[:, :], xt[:, cut], om_a[:, :], agg_s[:, :],
                                                             ALU.mult, ALU.add)
                    else:
                        ve.wait_ge(mm_done, k * NU + (NU * (NCH * p + 2)))
                        ve.wait_ge(y_ready, k + (NCH * p + 1))
                        ins = nc.vector.scalar_tensor_tensor(agg_s[:, :], psum[:, parity, :], 2.0, xt[:, cut],
                                                             ALU.mult, ALU.subtract)
                    ins.then_inc(agg_dve, 1)

                def ys_free(k, parity):
                    wait_some(ve, x_stored, before(LN_PASSES, p, k) * 16)
                    if p == 5:
                        wait_some(ve, xn_copied, k)
                    if p in FOLD_PASSES:
                        n = NA * 16 * (NCH // 2 * FOLD_PASSES.index(p) + parity)
                        for done in (folded, folded_whole):
                            wait_some(ve, done[1 - parity], (k - parity) * (NA * 8) + n)
                    else:
                        for done in (folded, folded_whole):
                            ve.wait_ge(done[1], NA * 16 * (NCH // 2 * len(FOLD_PASSES)))
                    if p < 5:
                        wait_some(ve, x_ready, before(X_PASSES, p, k))

                def layernorm(k, p_index, src):
                    ve.wait_ge(rstd_ready, k + (p_index + 1))
                    for t in range(TPC):
                        last = nc.vector.tensor_scalar(ys[:, t, :], src[:, t, :], mv[:, t, 0:1],
                                                       rstd[:, t:t + 1], ALU.subtract, ALU.mult)
                    last.then_inc(ys_ready, 1)
                    split(k)

                def split(k):
                    if p in FOLD_PASSES:
                        ve.wait_ge(ys_ready, k + (NCH * p + 1))
                        nc.vector.tensor_copy(yp[:, :, 0, :], ys[:, 0:4:2, :]).then_inc(ys_high, 1)
                        ve.wait_ge(ys_high, k + (nth(FOLD_PASSES, p, 0) + 1))
                        nc.vector.tensor_tensor(yp[:, :, 1, :], ys[:, 0:4:2, :], yp[:, :, 0, :].bitcast(fp32),
                                                ALU.subtract).then_inc(ys_split, 1)

                def residual(k, parity):
                    ve.wait_ge(xr_in[parity], k * 8 + (16 - 8 * parity + 8 * NCH * RES_PASSES.index(p)))

                def epilogue(k, parity, stage):
                    if stage == 0:
                        state[0] = Steps(ve, post, k * POST_STEPS[kind] + post_base)
                    steps = state[0]
                    seen = k + (NCH * p + 2)
                    if stage == 0:
                        ve.wait_ge(y_ready, seen)
                        if kind == "in":
                            for t in range(TPC):
                                tile = bass.ds(k * TPC + t, 1)
                                last = nc.vector.scalar_tensor_tensor(
                                    rs[:, t, :], psum[:, 2, t * D:(t + 1) * D], inv_r[:, tile],
                                    row(res[:, tile, :]), ALU.mult, ALU.add)
                            last.then_inc(y_used, 1)
                            ve.wait_ge(y_used, seen)
                            moments(steps, rs, TPC)
                        elif kind == "l1":
                            for t in range(TPC):
                                tile = bass.ds(k * TPC + t, 1)
                                last = nc.vector.scalar_tensor_tensor(
                                    rs[:, t, :], psum[:, 2, t * D:(t + 1) * D], inv_1[:, tile], b1_s[:, :],
                                    ALU.mult, ALU.add)
                            last.then_inc(y_used, 1)
                            ve.wait_ge(y_used, seen)
                            residual(k, parity)
                            steps.inc(nc.vector.scalar_tensor_tensor(rs[:, :, :], rs[:, :, :], 0.0,
                                                                     xr[:, parity], ALU.max, ALU.add))
                            steps.wait()
                            ve.sem_inc(xr_used, 1)
                            moments(steps, rs, TPC)
                        elif kind == "cheb1":
                            ys_free(k, parity)
                            nc.vector.tensor_copy(ys[:, :, :].rearrange("p t d -> p (t d)"), psum[:, 2, :])\
                              .then_inc(ys_ready, 1)
                            split(k)
                            ve.sem_inc(y_used, 1)
                        else:
                            for t in range(TPC):
                                last = nc.vector.tensor_tensor(rs[:, t, :], psum[:, 2, t * D:(t + 1) * D],
                                                               b2_s[:, (p - 3) // 2, :], ALU.add)
                            last.then_inc(y_used, 1)
                            ve.wait_ge(y_used, seen)
                            if p == 5:
                                wait_some(ve, x_ready, before(X_PASSES, p, k))
                            nc.vector.tensor_scalar(ns[:, :, :], rs[:, :, :], 0.0, None, ALU.min).then_inc(elu_in, 1)
                            ve.wait_ge(elu_in, k + (before(ELU_PASSES, p, 0) + 1))
                            steps.inc(nc.vector.tensor_scalar(rs[:, :, :], rs[:, :, :], 0.0, None, ALU.max))
                    elif stage == 1:
                        if kind in ("in", "l1"):
                            ys_free(k, parity)
                            layernorm(k, before(LN_PASSES, p, 0), rs)
                        elif kind == "cheb2":
                            ys_free(k, parity)
                            steps.wait()
                            ve.wait_ge(elu_out, k + (before(ELU_PASSES, p, 0) + 1))
                            nc.vector.scalar_tensor_tensor(ys[:, :, :], ns[:, :, :], -1.0, rs[:, :, :],
                                                           ALU.add, ALU.add).then_inc(ys_ready, 1)
                            split(k)
                        elif kind == "cheb2f":
                            steps.wait()
                            ve.wait_ge(elu_out, k + (before(ELU_PASSES, p, 0) + 1))
                            steps.inc(nc.vector.scalar_tensor_tensor(rs[:, :, :], ns[:, :, :], -1.0, rs[:, :, :],
                                                                     ALU.add, ALU.add))
                            steps.wait()
                            residual(k, parity)
                            steps.inc(nc.vector.tensor_tensor(rs[:, :, :], rs[:, :, :], xr[:, parity], ALU.add))
                            steps.wait()
                            ve.sem_inc(xr_used, 1)
                            moments(steps, rs, TPC)
                    elif stage == 2 and kind == "cheb2f":
                        steps = state[0] = Steps(ve, post, k * POST_STEPS[kind] + post_base)
                        steps.n = POST_STEPS[kind] - 1
                        ys_free(k, parity)
                        layernorm(k, before(LN_PASSES, p, 0), rs)
                        ve.wait_ge(ys_ready, k + (NCH * p + 1))
                        for t in range(TPC):
                            last = nc.vector.tensor_tensor_reduce(out=rs[:, t, :], in0=ys[:, t, :],
                                                                  in1=ys[:, t, :],
                                                                  scale=1.0, scalar=0.0, op0=ALU.mult, op1=ALU.add,
                                                                  accum_out=ss[:, t:t + 1])
                        steps.inc(last)
                        steps.wait()
                        nc.vector.tensor_scalar(ss[:, :], ss[:, :], NORM_MIN2, None, ALU.max).then_inc(ss_ready, 1)
                    elif stage == 3:
                        if kind == "cheb2f":
                            ve.wait_ge(rn_ready, k + 1)
                            for t in range(TPC):
                                last = nc.vector.tensor_scalar(ns[:, t, :], ys[:, t, :], rn[:, t:t + 1], None,
                                                               ALU.mult)
                            last.then_inc(ns_ready, 1)
                        assert steps.n == POST_STEPS[kind], (kind, steps.n)

                state = [None]

                return aggregate, epilogue

            post_base = 0
            aggregate, epilogue = None, None
            for p in range(6):
                last_aggregate, last_epilogue = aggregate, epilogue
                aggregate, epilogue = pass_steps(p, post_base)

                def chunk(k, parity):
                    first_of_all = p == 0 and isinstance(k, int) and k == 0
                    if first_of_all:
                        ve.wait_ge(o_pe, 2 * NO + FR)
                        ve.wait_ge(o_act, OT * (2 * NO + FR))
                    for i in range(2 if first_of_all else 0, 2):
                        transpose(p, k, i)
                    late = p == 5 and not (isinstance(k, int) and k < 2)
                    if late:
                        epilogue(k - 2, parity, 2)
                    for i in range(2, 4):
                        transpose(p, k, i)
                    if late:
                        epilogue(k - 2, parity, 3)
                    if isinstance(k, int) and k == 0:
                        if p > 0:
                            last_aggregate(NCH - 1, 1)
                        transpose(p, k, 4)
                        if p > 0:
                            for stage in range(4):
                                last_epilogue(NCH - 1, 1, stage)
                        else:
                            row_scales()
                        for i in range(5, NU):
                            transpose(p, k, i)
                        return
                    aggregate(k - 1, 1 - parity)
                    for i in range(4, NU - 1):
                        transpose(p, k, i)
                    epilogue(k - 1, 1 - parity, 0)
                    epilogue(k - 1, 1 - parity, 1)
                    transpose(p, k, NU - 1)
                    if p < 5:
                        epilogue(k - 1, 1 - parity, 2)
                        epilogue(k - 1, 1 - parity, 3)

                pairs(ve, chunk)
                post_base += NCH * POST_STEPS[KINDS[p]]
            epilogue(NCH - 2, 0, 2)
            epilogue(NCH - 2, 0, 3)
            aggregate(NCH - 1, 1)
            for stage in range(4):
                epilogue(NCH - 1, 1, stage)

            ve.wait_ge(xn_copied, NCH)
            ve.wait_ge(x_ready, 4 * NCH)
            ve.wait_ge(xt_done, 4 * NCH + 1)
            h_base = 0
            for layer in range(2):
                R0 = NT * layer
                G0 = NT // 2 * layer

                def mask(g, tt, q):
                    ve.wait_ge(a_loaded[tt][q], g * 16 + 16 * (NT // 4 * layer + 1))
                    part = ring[:, tt, q * 2 * CH:(q + 1) * 2 * CH]
                    nc.vector.tensor_scalar(part, part, 0.0, NEG, ALU.is_le, ALU.mult).then_inc(masked, 1)

                def query_low(g, tt):
                    ve.wait_ge(qh_ready, g * 4 + (R0 + tt + 1))
                    nc.vector.tensor_tensor(q_l[:, tt % 2, :], q_f[:, 1, :], q_h[:, tt % 2, :].bitcast(fp32),
                                            ALU.subtract).then_inc(ql_ready, 1)

                def finish_rows(g, tt):
                    G = g * 2 + (tt // 2 - 2)
                    steps = Steps(ve, h_done, G * H_STEPS[layer] + h_base)
                    wait_apart(ve, ot_ready, G + (G0 + 2))
                    steps.inc(nc.vector.tensor_reduce(out=rsum[:, :], in_=esum[:, bass.ds(G * 2, 2), :],
                                                      axis=AX.X, op=ALU.add))
                    steps.wait()
                    steps.inc(nc.vector.reciprocal(rsum[:, :], rsum[:, :]))
                    steps.wait()
                    for t in range(2):
                        last = nc.vector.tensor_scalar(hr[:, t, :], psum[:, 7, t * D:(t + 1) * D],
                                                       rsum[:, t:t + 1], None, ALU.mult)
                    last.then_inc(h_ready, 1)
                    ve.wait_ge(h_ready, G + (G0 + 1))
                    if layer == 0:
                        ve.wait_ge(hy_free, G + 1)
                        nc.vector.scalar_tensor_tensor(hy[:, :, :], hr[:, :, :], LEAK, hr[:, :, :],
                                                       ALU.mult, ALU.max).then_inc(hs_ready, 1)
                        ve.wait_ge(hs_ready, G + 1)
                        for t in range(2):
                            last = nc.vector.tensor_tensor_reduce(out=hr[:, t, :], in0=hy[:, t, :], in1=hy[:, t, :],
                                                                  scale=1.0, scalar=0.0, op0=ALU.mult, op1=ALU.add,
                                                                  accum_out=ss[:, t:t + 1])
                        steps.inc(last)
                        steps.wait()
                        nc.vector.tensor_scalar(ss[:, 0:2], ss[:, 0:2], NORM_MIN2, None, ALU.max)\
                          .then_inc(hss_ready, 1)
                    else:
                        steps.inc(nc.vector.scalar_tensor_tensor(hy[:, :, :], hr[:, :, :], LEAK, hr[:, :, :],
                                                                 ALU.mult, ALU.max))
                        steps.wait()
                        ve.wait_ge(x3_loaded, G * 16 + 16)
                        steps.inc(nc.vector.tensor_tensor(hy[:, :, :], hy[:, :, :], x3_s[:, :, :], ALU.add))
                        steps.wait()
                        moments(steps, hy, 2)
                    assert steps.n == H_STEPS[layer], steps.n

                def finish_norm(G):
                    if layer == 0:
                        ve.wait_ge(hrn_ready, G + 1)
                        for t in range(2):
                            last = nc.vector.tensor_scalar(hz[:, t, :], hy[:, t, :], rn[:, t:t + 1], None, ALU.mult)
                        last.then_inc(hns_ready, 1)
                    else:
                        ve.wait_ge(rstd_ready, G + (3 * NCH + 1))
                        ve.wait_ge(out_free, G + 1)
                        for t in range(2):
                            last = nc.vector.tensor_scalar(hz[:, t, :], hy[:, t, :], mv[:, t, 0:1], rstd[:, t:t + 1],
                                                           ALU.subtract, ALU.mult)
                        last.then_inc(out_ready, 1)

                def step(g, tt, scores, back, ends):
                    more = scores and not (isinstance(g, int) and g * 4 + tt == NT - 1)
                    if scores:
                        ve.wait_ge(masked, g * 16 + 4 * (R0 + tt + 1))
                    for q in range(4):
                        if scores:
                            wait_apart(ve, s_ready, g * 16 + (4 * (R0 + tt) + q + 1))
                            b = 2 * (q % 2)
                            part = ring[:, tt, q * 2 * CH:(q + 1) * 2 * CH]
                            nc.vector.tensor_tensor_reduce(
                                out=part, in0=psum[:, b:b + 2, :].rearrange("p b c -> p (b c)"), in1=part,
                                scale=1.0, scalar=-3e38, op0=ALU.add, op1=ALU.max,
                                accum_out=mx[:, tt % 2, q:q + 1]).then_inc(s_masked, 1)
                        if scores and q == 3:
                            ve.wait_ge(s_masked, g * 16 + (4 * (R0 + tt) + 6))
                            nc.vector.tensor_reduce(out=nmx[:, tt:tt + 1], in_=mx[:, tt % 2, :], axis=AX.X,
                                                    op=ALU.max, negate=True).then_inc(max_ready, 1)
                        if back:
                            for w in (2 * q, 2 * q + 1):
                                ve.wait_ge(ev_high, g * 32 + (8 * (R0 + tt - 2) + w + 1))
                                cut = pt_cut(w, tt)
                                nc.vector.tensor_tensor(pt_l[cut], psum[:, 4 + w % 2, :].rearrange(
                                    "p (u i) -> p u i", i=P), pt_h[cut].bitcast(fp32), ALU.subtract)\
                                  .then_inc(ev_low, 1)
                        if more:
                            mask(*next_tile(g, tt), q)
                            if q == 1:
                                query_low(*next_tile(g, tt))
                        if ends and tt % 2 and q == 1:
                            finish_rows(g, tt)
                        if q == 2 and normed(g, tt, ends) is not None:
                            finish_norm(normed(g, tt, ends))
                for q in range(4):
                    mask(0, 0, q)
                for part in range(4):
                    cut = slice(part * (N // 4), (part + 1) * (N // 4))
                    ve.wait_ge(k_high, 4 * layer + part + 1)
                    nc.vector.tensor_tensor(k_l[:, cut], xt[:, cut], k_h[:, cut].bitcast(fp32), ALU.subtract)\
                      .then_inc(k_split, 1)
                    if part == 1:
                        query_low(0, 0)
                attention(ve, step)
                h_base += NT // 2 * H_STEPS[layer]

        @block.scalar
        def _(act):
            act.sem_inc(o_act, OT * FR)
            act.sem_inc(xt_done, 1)
            act.sem_inc(hk_ready, 1)
            act.wait_ge(loaded[0], 16)
            act.dma_start(w_out_s[:, :], w_out).then_inc(consts, 16)
            act.dma_start(w_in_s[:, :], w_in).then_inc(consts, 16)
            act.dma_start(w1_s[:, :], w1t).then_inc(consts, 16)
            act.dma_start(w2_s[:, 0], w2a.rearrange("j d e -> d j e")).then_inc(consts, 16)
            act.dma_start(w2_s[:, 1], w2b.rearrange("j d e -> d j e")).then_inc(consts, 16)
            act.dma_start(b1_s[:, :], b1.partition_broadcast(P)).then_inc(consts, 16)
            act.dma_start(b2_s[:, 0], b2a.partition_broadcast(P)).then_inc(consts, 16)
            act.dma_start(b2_s[:, 1], b2b.partition_broadcast(P)).then_inc(consts, 16)
            act.dma_start(sc[:, 0:1], alpha.partition_broadcast(P)).then_inc(consts, 16)
            act.dma_start(sc[:, 1:2], beta1.partition_broadcast(P)).then_inc(consts, 16)
            act.dma_start(sc[:, 2:3], beta2.partition_broadcast(P)).then_inc(consts, 16)
            for sweep in range(2):
                for n in range(NO):
                    act.wait_ge(loaded[n % FR], sweep * (LOADS_O // 2) + 16 * (n // FR + 1))
                    tile = ring[:, n % FR, :].rearrange("p (t c) -> p t c", t=OT)
                    for t in range(OT):
                        act.wait_ge(o_act, sweep * (OT * NO) + (OT * (FR + n) + t))
                        nc.scalar.activation(junk, tile[:, t, :], ACT.Copy,
                                             accum_out=rowp[:, sweep, n * OT + t:n * OT + t + 1]).then_inc(o_act, 1)
                act.wait_ge(o_mm, sweep * 5 + 1)
                act.wait_ge(o_dve, sweep * NO + (NO + FR))
                nc.scalar.activation(col_s, psum[:, 4:8, :].rearrange("p b c -> p (b c)"), ACT.Copy)\
                  .then_inc(o_copied, 1)
                if sweep == 1:
                    act.wait_ge(x_in, 16 * NA)
                    for kk in range(2):
                        for t in (0, 2):
                            b0 = (kk * TPC + t) * NA
                            nc.scalar.activation(xp[:, 0, kk, :, t // 2, 0, :], x_folded[:, b0:b0 + NA, :], ACT.Copy)\
                              .then_inc(x_high, 1)
                act.wait_ge(o_pe, sweep * NO + (NO + FR))
                for bank in range(4):
                    nc.scalar.activation(out_s[:, bank * CH:(bank + 1) * CH], psum[:, bank, :], ACT.Copy)\
                      .then_inc(o_copied, 1)
            act.wait_ge(consts, 16 * N_CONSTS)

            def high_part(p, k, u):
                act.wait_ge(transposed, k * NU + (NU * NCH * p + ORDER.index(u) + 1 + LR))
                act.wait_ge(mm_done, k * NU + (NU * NCH * p + u + 1 - 2 * HR + NU))
                nc.scalar.activation(high_tile(u), split_tile(u), ACT.Copy).then_inc(high_made, 1)

            def pass_steps(p):
                kind = KINDS[p]

                def stage(k, parity):
                    cut = bass.ds(k * CH, CH)
                    act.wait_ge(y_ready, k + (NCH * p + 1))
                    if kind in ("cheb2", "cheb2f"):
                        act.wait_ge(xt_done, before(X_PASSES, p, 0) + 1)
                        nc.scalar.activation(st0[:, :], xt[:, cut], ACT.Copy)
                        act.wait_ge(agg_act, NCH * p)
                        nc.scalar.activation(st1[:, :], t1t[:, cut], ACT.Copy).then_inc(agg_act, 1)
                        return
                    act.wait_ge(mm_done, k * NU + (NU * (NCH * p + 2)))
                    if kind == "l1":
                        nc.scalar.activation(agg_s[:, :], psum[:, parity, :], ACT.Identity, scale=sc[:, 0:1])\
                          .then_inc(agg_act, 1)
                    elif kind == "in":
                        nc.scalar.activation(agg_s[:, :], psum[:, parity, :], ACT.Copy).then_inc(agg_act, 1)
                    else:
                        wait_some(act, agg_act, NCH * p)
                        nc.scalar.activation(t1t[:, cut], psum[:, parity, :], ACT.Copy)
                        nc.scalar.activation(agg_s[:, :], psum[:, parity, :], ACT.Copy).then_inc(agg_act, 1)

                def elu(k):
                    if p in ELU_PASSES:
                        act.wait_ge(elu_in, k + (before(ELU_PASSES, p, 0) + 1))
                        nc.scalar.activation(ns[:, :, :], ns[:, :, :], ACT.Exp).then_inc(elu_out, 1)

                def columns(k):
                    if p in X_PASSES:
                        wait_apart(act, x_ready, k + (before(X_PASSES, p, 0) + 1))
                        nc.scalar.activation(xt[:, bass.ds(k * CH, CH)], psum[:, 3, :], ACT.Copy).then_inc(xt_done, 1)

                def rows_out(k):
                    act.wait_ge(ys_ready, NCH * p + k + 1)
                    if p in LN_PASSES:
                        x_d = (x1_d, x2_d, x3_d)[LN_PASSES.index(p)]
                        rows = x_d[k * CH:(k + 1) * CH, :].rearrange("(t p) d -> p t d", p=P)
                        act.dma_start(rows, ys[:, :, :]).then_inc(x_stored, 16)
                    if p in FOLD_PASSES:
                        m, kk = divmod(k, 2)
                        for s in range(NA):
                            act.dma_start(xw[Q * m:Q * (m + 1), (p + 1) % 2, kk, s], ys[Q * s:Q * (s + 1), 1:4:2, :])\
                              .then_inc(folded_whole[kk], 16)

                return stage, elu, columns, rows_out

            stage, elu, columns, rows_out = None, None, None, None
            for p in range(6):
                for k in range(NCH):
                    high_part(p, k, 0)
                    high_part(p, k, 2)
                    late = p == 5 and k > 1
                    if (p > 0 or k > 1) and not late:
                        columns((k - 2) % NCH)
                    if k == 1 or p == 0 and k == 0:
                        stage, elu, columns, rows_out = pass_steps(p)
                    if p > 0 or k > 0:
                        stage((k - 1) % NCH, (k - 1) % 2)
                    high_part(p, k, 4)
                    if late:
                        rows_out(k - 2)
                        columns(k - 2)
                    if p > 0 or k > 0:
                        elu((k - 1) % NCH)
                    high_part(p, k, 6)
                    if (p > 0 or k > 0) and not (p == 5 and k > 0):
                        rows_out((k - 1) % NCH)
            rows_out(NCH - 2)
            columns(NCH - 2)
            stage(NCH - 1, 1)
            elu(NCH - 1)
            rows_out(NCH - 1)
            columns(NCH - 1)

            act.wait_ge(xt_done, 4 * NCH + 1)
            act.wait_ge(xn_copied, NCH)
            for layer in range(2):
                R0 = NT * layer
                G0 = NT // 2 * layer
                def query_high(g, tt):
                    act.wait_ge(q_made, g * 4 + (R0 + tt + 1))
                    nc.scalar.activation(q_h[:, tt % 2, :], q_f[:, 1, :], ACT.Copy).then_inc(qh_ready, 1)

                def step(g, tt, scores, back, ends):
                    more = scores and not (isinstance(g, int) and g * 4 + tt == NT - 1)
                    exp = (scores or tt == 0) and not (isinstance(g, int) and g * 4 + tt == 0)
                    G = g * 2 + (tt // 2 - 2)
                    for w in range(8):
                        if exp and w % 2 == 0:
                            q = w // 2
                            if q == 0:
                                act.wait_ge(max_ready, g * 4 + (R0 + tt))
                            slot = (tt - 1) % 4
                            part = ring[:, slot, q * 2 * CH:(q + 1) * 2 * CH]
                            nc.scalar.activation(part, part, ACT.Exp, bias=nmx[:, slot:slot + 1],
                                                 accum_out=row(esum[:, bass.ds(g * 4 + (tt - 1), 1), q:q + 1]))\
                              .then_inc(exp_done, 1)
                        if w == 2 and more:
                            query_high(*next_tile(g, tt))
                        if not back:
                            continue
                        if w == 0 and isinstance(g, int) and g == 0 and tt == 2:
                            act.wait_ge(v_split, 2 * (layer + 1))
                        act.wait_ge(tp_done, g * 32 + (8 * (R0 + tt - 2) + w + 1 + 8 * FR))
                        nc.scalar.activation(pt_h[pt_cut(w, tt)], psum[:, 4 + w % 2, :].rearrange(
                            "p (u i) -> p u i", i=P), ACT.Copy).then_inc(ev_high, 1)
                    if ends and tt % 2 == 0:
                        act.wait_ge(pv_done, G + (G0 + 1))
                        act.wait_ge(ot_ready, G + (G0 + 1))
                        nc.scalar.activation(o_s[:, :], psum[:, 6, 0:PT2], ACT.Copy).then_inc(o_staged, 1)
                    G = normed(g, tt, ends)
                    if G is not None and layer == 0:
                        act.wait_ge(hk_free, G + 1)
                        act.wait_ge(hx_ready, G + 1)
                        nc.scalar.activation(hk[:, :], psum[:, 7, PT2:2 * PT2], ACT.Copy).then_inc(hk_ready, 1)

                for part in range(4):
                    if layer == 1:
                        act.wait_ge(hk_loaded[part], 16)
                    cut = slice(part * (N // 4), (part + 1) * (N // 4))
                    nc.scalar.activation(k_h[:, cut], xt[:, cut], ACT.Copy).then_inc(k_high, 1)
                    if part == 1:
                        query_high(0, 0)
                if layer == 1:
                    act.wait_ge(hv_loaded, 16)
                for part in range(2):
                    half = slice(part * (NT // 2), (part + 1) * (NT // 2))
                    nc.scalar.activation(v_h[:, half, :], xn[:, half, :], ACT.Copy).then_inc(v_high, 1)
                attention(act, step)

        @block.gpsimd
        def _(pool):
            nc.gpsimd.memset(ones[:, :], 1.0).then_inc(ident_ready, 1)
            nc.gpsimd.memset(mhalf[:, :], -0.5).then_inc(ident_ready, 1)
            nc.gpsimd.memset(ident[:, :], 0.0).then_inc(ident_ready, 1)
            pool.wait_ge(ident_ready, 3)
            nc.gpsimd.affine_select(out=ident[:, :], in_=ident[:, :], compare_op=ALU.not_equal, fill=1.0,
                                    base=0, pattern=[[-1, P]], channel_multiplier=1).then_inc(ident_ready, 1)
            pool.sem_inc(hy_free, 1)
            pool.sem_inc(hk_free, 1)
            for kk in range(2):
                for t in (1, 3):
                    b0 = (kk * TPC + t) * NA
                    pool.wait_ge(o_pe, FR + 2 * kk + t // 2 + 1)
                    for a in range(NA):
                        rows = x[RANGE * a + Q * b0:RANGE * a + Q * (b0 + NA), :]
                        pool.dma_start(xw[Q * a:Q * (a + 1), 0, kk, :, t // 2, :],
                                       rows.rearrange("(s q) d -> q s d", q=Q)).then_inc(x_whole, 16)
            for a in range(NA):
                pool.wait_ge(o_pe, FR + 4 + a + 1)
                pool.dma_start(x_folded[Q * a:Q * (a + 1)], x[RANGE * a:RANGE * (a + 1), :]
                               .rearrange("(b q) d -> q b d", q=Q)).then_inc(x_in, 16)
            pool.wait_ge(x_in, 16 * NA)
            for kk in range(2):
                for t in (0, 2):
                    b0 = (kk * TPC + t) * NA
                    pool.wait_ge(x_high, 2 * kk + t // 2 + 1)
                    nc.gpsimd.tensor_tensor(xp[:, 0, kk, :, t // 2, 1, :], x_folded[:, b0:b0 + NA, :],
                                            xp[:, 0, kk, :, t // 2, 0, :].bitcast(fp32), ALU.subtract)\
                      .then_inc(x_split, 1)

            def low_part(p, k, u):
                pool.wait_ge(high_made, NU // 2 * (NCH * p + k) + u // 2 + 1)
                nc.gpsimd.tensor_tensor(low_tile(u), split_tile(u), high_tile(u).bitcast(fp32), ALU.subtract)\
                  .then_inc(low_made, 1)

            def variance(p, k):
                if p in LN_PASSES:
                    pool.wait_ge(var_ready, nth(LN_PASSES, p, k) + 1)
                    nc.gpsimd.tensor_tensor(rstd[:, :], var_s[:, :], mhalf[:, :], ALU.pow).then_inc(rstd_ready, 1)

            def fold(p, k):
                m, kk = divmod(k, 2)
                if p in FOLD_PASSES:
                    pool.wait_ge(ys_split, nth(FOLD_PASSES, p, k) + 1)
                    for s in range(NA):
                        pool.dma_start(xp[Q * m:Q * (m + 1), (p + 1) % 2, kk, s], yp[Q * s:Q * (s + 1)])\
                          .then_inc(folded[kk], 16)
                if p == 5:
                    pool.wait_ge(ss_ready, k + 1)
                    nc.gpsimd.tensor_tensor(rn[:, :], ss[:, :], mhalf[:, :], ALU.pow).then_inc(rn_ready, 1)
                    pool.wait_ge(ys_ready, NCH * p + k + 1)
                    nc.gpsimd.tensor_copy(xn[:, k * TPC:(k + 1) * TPC, :], ys[:, :, :]).then_inc(xn_copied, 1)

            for p in range(6):
                for k in range(NCH):
                    low_part(p, k, 0)
                    if p == 5 and k > 1:
                        fold(p, k - 2)
                    low_part(p, k, 2)
                    if k > 0 or p - 1 not in LN_PASSES:
                        low_part(p, k, 4)
                    if k > 0:
                        variance(p, k - 1)
                        low_part(p, k, 6)
                        if p < 5:
                            fold(p, k - 1)
                        continue
                    if p > 0:
                        variance(p - 1, NCH - 1)
                        fold(p - 1, NCH - 1)
                    if p - 1 in LN_PASSES:
                        low_part(p, k, 4)
                    low_part(p, k, 6)
            fold(5, NCH - 2)
            variance(5, NCH - 1)
            fold(5, NCH - 1)
            for layer in range(2):
                R0 = NT * layer

                def query(g, tt):
                    if not (layer == 0 and isinstance(g, int) and g * 4 + tt == 0):
                        pool.wait_ge(ql_ready, g * 4 + (R0 + tt))
                    cut = bass.ds(g * (4 * P) + tt * P, P)
                    nc.gpsimd.tensor_tensor(q_f[:, 0, :], k_h[:, cut].bitcast(fp32), k_l[:, cut].bitcast(fp32),
                                            ALU.add).then_inc(q_raw, 1)
                    wait_apart(pool, q_raw, g * 4 + (R0 + tt + 1))
                    nc.gpsimd.tensor_scalar(q_f[:, 1, :], q_f[:, 0, :], sc[:, 1 + layer:2 + layer], None, ALU.mult)\
                      .then_inc(q_made, 1)

                def values_low(part):
                    pool.wait_ge(v_high, 2 * layer + part + 1)
                    if layer == 0:
                        pool.wait_ge(x_stored, 16 * 3 * NCH)
                    half = slice(part * (NT // 2), (part + 1) * (NT // 2))
                    nc.gpsimd.tensor_tensor(v_l[:, half, :], xn[:, half, :], v_h[:, half, :].bitcast(fp32),
                                            ALU.subtract).then_inc(v_split, 1)

                def x3_rows(G):
                    return bass.ds(G * PT2, PT2)

                def step(g, tt, scores, back, ends):
                    G = g * 2 + (tt // 2 - 2)
                    if scores and not (isinstance(g, int) and g * 4 + tt == NT - 1):
                        query(*next_tile(g, tt))
                    if isinstance(g, int) and g == 0 and tt < 2:
                        values_low(tt)
                    if ends and tt % 2 and layer == 0:
                        wait_apart(pool, hs_ready, G + 1)
                        pool.dma_start(h_d[x3_rows(G), :].rearrange("(t p) d -> p t d", p=P), hy[:, :, :])\
                          .then_inc(h_stored, 16)
                        pool.wait_ge(hss_ready, G + 1)
                        nc.gpsimd.tensor_tensor(rn[:, 0:2], ss[:, 0:2], mhalf[:, 0:2], ALU.pow).then_inc(hrn_ready, 1)
                        pool.wait_ge(h_stored, G * 16 + 16)
                        pool.sem_inc(hy_free, 1)
                    if ends and tt % 2 and layer == 1:
                        pool.wait_ge(var_ready, G + (3 * NCH + 1))
                        nc.gpsimd.tensor_tensor(rstd[:, 0:2], var_s[:, 0:2], mhalf[:, 0:2], ALU.pow)\
                          .then_inc(rstd_ready, 1)
                        if not (isinstance(g, int) and g * 2 + tt // 2 - 2 == NT // 2 - 1):
                            wait_apart(pool, rstd_ready, G + (3 * NCH + 1))
                            pool.dma_start(x3_s[:, :, :], x3_d[x3_rows(G + 1), :].rearrange("(t p) d -> p t d", p=P))\
                              .then_inc(x3_loaded, 16)
                    G = normed(g, tt, ends)
                    if G is not None and layer == 0:
                        wait_apart(pool, hk_ready, G + 2)
                        pool.dma_start(hk_d[:, x3_rows(G)], hk[:, :]).then_inc(hk_stored, 16)
                        pool.wait_ge(hk_stored, G * 16 + 16)
                        pool.sem_inc(hk_free, 1)
                    if G is not None and layer == 1:
                        wait_apart(pool, out_ready, G + 1)
                        pool.dma_start(out[x3_rows(G), :].rearrange("(t p) d -> p t d", p=P), hz[:, :, :])\
                          .then_inc(out_done, 16)
                        pool.wait_ge(out_done, G * 16 + 16)
                        pool.sem_inc(out_free, 1)

                pool.wait_ge(k_split, 4 * layer + 1)
                if layer == 1:
                    pool.sem_inc(out_free, 1)
                    pool.dma_start(x3_s[:, :, :], x3_d[0:PT2, :].rearrange("(t p) d -> p t d", p=P))\
                      .then_inc(x3_loaded, 16)
                query(0, 0)
                attention(pool, step)
            pool.wait_ge(out_done, 16 * (NT // 2))
    return nc


_INS = ["x", "adj", "L0_gnn_W_in", "L0_gnn_W_out", "L1_gnn_alpha", "L1_gnn_W", "L1_gnn_b",
        "L2_gnn_W0", "L2_gnn_b0", "L2_gnn_W1", "L2_gnn_b1", "L3_gnn_beta1", "L3_gnn_beta2"]


def kernel(**inputs):
    import numpy as np
    import concourse.bacc as bacc
    from concourse import mybir
    from concourse.bass_utils import run_bass_kernel_spmd

    nc = bacc.Bacc("TRN2", target_bir_lowering=False, num_devices=1)
    arrays, args = {}, []
    for name in _INS:
        a = np.asarray(inputs[name])
        if name == "L1_gnn_W":
            a = a.T
        a = np.ascontiguousarray(a)
        arrays[f"in_{name}_dram"] = a
        args.append(nc.dram_tensor(f"in_{name}_dram", a.shape, mybir.dt.from_np(a.dtype),
                                   kind="ExternalInput").ap())
    out = nc.dram_tensor("out_dram", (4096, 128), mybir.dt.float32, kind="ExternalOutput").ap()
    build_gnn_stack(nc, *args, out)
    r = run_bass_kernel_spmd(nc, [arrays], core_ids=[0])
    return r.results[0]["out_dram"]
```
